# Optimizing a Trainium2 kernel written in Bass

```python
import numpy as np
import jax
import jax.numpy as jnp

def _softmax(x, axis=-1):
    return jax.nn.softmax(x, axis=axis)

def _gelu(x):
    return jax.nn.gelu(x, approximate=True)

def _silu(x):
    return jax.nn.silu(x)

def _sigmoid(x):
    return jax.nn.sigmoid(x)

def _layernorm(x, axis=-1, eps=1e-05):
    m = jnp.mean(x, axis=axis, keepdims=True)
    v = jnp.var(x, axis=axis, keepdims=True)
    return (x - m) / jnp.sqrt(v + eps)

def _scatter_add(tgt, idx, src, axis=0):
    return tgt.at[idx].add(src)

def _segment_sum(src, seg, n):
    return jax.ops.segment_sum(src, seg, n)
kernel_name = 'mk_gnn_ffn_d1_gnn_r32_ba2845'

def setup_inputs(seed: int=0):
    np.random.seed(seed)
    _w = jnp.asarray

    def _rec_inputs():
        import jax
        import jax.numpy as jnp
        _gk = jax.random.key(seed)
        x = -0.0003713 + 1 * jax.random.normal(jax.random.fold_in(_gk, 1), (3125, 256), jnp.float32)
        _s = jax.random.randint(jax.random.fold_in(_gk, 2), (25000,), 0, 3125, jnp.int32)
        _d = jax.random.randint(jax.random.fold_in(_gk, 3), (25000,), 0, 3125, jnp.int32)
        _loop = jnp.arange(3125, dtype=jnp.int32)
        src = jnp.concatenate([_s, _d, _loop])
        dst = jnp.concatenate([_d, _s, _loop])
        _o = jnp.argsort(dst, stable=True)
        src = src[_o]
        dst = dst[_o]
        return (x, src, dst)
    x, src, dst = _rec_inputs()

    def _L0_gnn_setup():
        import jax, jax.numpy as jnp
        import numpy as np
        N_NODES = 50000
        N_EDGES = 25000
        IN_CH = 256
        OUT_CH = 64
        HEADS = 4
        NEG_SLOPE = 0.2
        key = jax.random.key(seed)
        k = jax.random.split(key, 7)
        x = jax.random.normal(k[0], (N_NODES, IN_CH), dtype=jnp.float32)
        edge_index = jax.random.randint(k[1], (2, N_EDGES), 0, N_NODES, dtype=jnp.int32)
        W = jax.random.normal(k[2], (IN_CH, HEADS * OUT_CH), dtype=jnp.float32) / np.sqrt(IN_CH)
        att_src = jax.random.normal(k[3], (HEADS, OUT_CH), dtype=jnp.float32) / np.sqrt(OUT_CH)
        att_dst = jax.random.normal(k[4], (HEADS, OUT_CH), dtype=jnp.float32) / np.sqrt(OUT_CH)
        bias = jnp.zeros((HEADS * OUT_CH,), dtype=jnp.float32)
        return {'x': x, 'edge_index': edge_index, 'W': W, 'att_src': att_src, 'att_dst': att_dst, 'bias': bias}
    _L0_gnn_all = _L0_gnn_setup()
    _L0_gnn_in = {k: v for k, v in _L0_gnn_all.items() if k in ('W', 'att_src', 'att_dst', 'bias')}
    del _L0_gnn_all

    def _L0_ffn_setup():
        import jax, jax.numpy as jnp
        import numpy as np
        E, D, H, TOP_K = (6, 256, 256, 2)
        ROUTER_H = D // 2
        key = jax.random.key(seed)
        ks = jax.random.split(key, 12)
        s = 1.0 / np.sqrt(D)
        sh = 1.0 / np.sqrt(H)
        sr = 1.0 / np.sqrt(ROUTER_H)
        return {'features': jax.random.normal(ks[0], (8, 128, D), dtype=jnp.float32), 'router_w1': jax.random.uniform(ks[1], (D, ROUTER_H), jnp.float32, -s, s), 'router_b1': jnp.zeros((ROUTER_H,), jnp.float32), 'router_w2': jax.random.uniform(ks[2], (ROUTER_H, E), jnp.float32, -sr, sr), 'router_b2': jnp.zeros((E,), jnp.float32), 'expert_w1': jax.random.uniform(ks[3], (E, D, H), jnp.float32, -s, s), 'expert_b1': jnp.zeros((E, H), jnp.float32), 'expert_w2': jax.random.uniform(ks[4], (E, H, H), jnp.float32, -sh, sh), 'expert_b2': jnp.zeros((E, H), jnp.float32), 'expert_w3': jax.random.uniform(ks[5], (E, H, D), jnp.float32, -sh, sh), 'expert_b3': jnp.zeros((E, D), jnp.float32)}
    _L0_ffn_all = _L0_ffn_setup()
    _L0_ffn_in = {k: v for k, v in _L0_ffn_all.items() if k in ('router_w1', 'router_b1', 'router_w2', 'router_b2', 'expert_w1', 'expert_b1', 'expert_w2', 'expert_b2', 'expert_w3', 'expert_b3')}
    del _L0_ffn_all
    return {'x': x, 'src': src, 'dst': dst, 'L0_gnn_W': _L0_gnn_in['W'], 'L0_gnn_att_src': _L0_gnn_in['att_src'], 'L0_gnn_att_dst': _L0_gnn_in['att_dst'], 'L0_gnn_bias': _L0_gnn_in['bias'], 'L0_ffn_router_w1': _L0_ffn_in['router_w1'], 'L0_ffn_router_b1': _L0_ffn_in['router_b1'], 'L0_ffn_router_w2': _L0_ffn_in['router_w2'], 'L0_ffn_router_b2': _L0_ffn_in['router_b2'], 'L0_ffn_expert_w1': _L0_ffn_in['expert_w1'], 'L0_ffn_expert_b1': _L0_ffn_in['expert_b1'], 'L0_ffn_expert_w2': _L0_ffn_in['expert_w2'], 'L0_ffn_expert_b2': _L0_ffn_in['expert_b2'], 'L0_ffn_expert_w3': _L0_ffn_in['expert_w3'], 'L0_ffn_expert_b3': _L0_ffn_in['expert_b3']}

def reference(x, src, dst, L0_gnn_W, L0_gnn_att_src, L0_gnn_att_dst, L0_gnn_bias, L0_ffn_router_w1, L0_ffn_router_b1, L0_ffn_router_w2, L0_ffn_router_b2, L0_ffn_expert_w1, L0_ffn_expert_b1, L0_ffn_expert_w2, L0_ffn_expert_b2, L0_ffn_expert_w3, L0_ffn_expert_b3):
    import jax
    import jax.numpy as jnp

    def _L0_gnn_ref(x, edge_index, W, att_src, att_dst, bias):
        import jax, jax.numpy as jnp
        import numpy as np
        N_NODES = 50000
        N_EDGES = 25000
        IN_CH = 256
        OUT_CH = 64
        HEADS = 4
        NEG_SLOPE = 0.2
        N = x.shape[0]
        loop = jnp.arange(N, dtype=edge_index.dtype)
        src = jnp.concatenate([edge_index[0], loop])
        dst = jnp.concatenate([edge_index[1], loop])
        h = (x @ W).reshape(N, HEADS, OUT_CH)
        a_src = jnp.einsum('nhc,hc->nh', h, att_src)
        a_dst = jnp.einsum('nhc,hc->nh', h, att_dst)
        alpha = a_src[src] + a_dst[dst]
        alpha = jax.nn.leaky_relu(alpha, NEG_SLOPE)
        amax = jax.ops.segment_max(alpha, dst, num_segments=N)
        amax = jnp.where(jnp.isfinite(amax), amax, 0.0)
        e = jnp.exp(alpha - amax[dst])
        denom = jax.ops.segment_sum(e, dst, num_segments=N)
        coef = e / (denom[dst] + 1e-16)
        msg = coef[..., None] * h[src]
        out = jax.ops.segment_sum(msg, dst, num_segments=N)
        out = out.reshape(N, HEADS * OUT_CH) + bias
        return jax.nn.relu(out)

    def _L0_ffn_ref(features, router_w1, router_b1, router_w2, router_b2, expert_w1, expert_b1, expert_w2, expert_b2, expert_w3, expert_b3):
        import jax, jax.numpy as jnp
        import numpy as np
        E, D, H, TOP_K = (6, 256, 256, 2)
        ROUTER_H = D // 2
        rh = jax.nn.relu(features @ router_w1 + router_b1)
        expert_logits = jax.nn.softmax(rh @ router_w2 + router_b2, axis=-1)
        top_w, top_i = jax.lax.top_k(expert_logits, TOP_K)
        routing_weights = jax.nn.softmax(top_w, axis=-1)
        h1 = jax.nn.relu(jnp.einsum('bsd,edh->bseh', features, expert_w1) + expert_b1)
        h2 = jax.nn.relu(jnp.einsum('bseh,ehf->bsef', h1, expert_w2) + expert_b2)
        expert_out = jnp.einsum('bsef,efo->bseo', h2, expert_w3) + expert_b3
        sel = jnp.take_along_axis(expert_out, top_i[:, :, :, None], axis=2)
        combined = jnp.sum(sel * routing_weights[..., None], axis=2)
        return combined
    edge_index = jnp.stack([src, dst])
    x = x + _L0_gnn_ref(_layernorm(x, axis=-1), edge_index, L0_gnn_W, L0_gnn_att_src, L0_gnn_att_dst, L0_gnn_bias)
    x = x + _L0_ffn_ref(_layernorm(x, axis=-1)[None], L0_ffn_router_w1, L0_ffn_router_b1, L0_ffn_router_w2, L0_ffn_router_b2, L0_ffn_expert_w1, L0_ffn_expert_b1, L0_ffn_expert_w2, L0_ffn_expert_b2, L0_ffn_expert_w3, L0_ffn_expert_b3)[0]
    return x

_drawn_inputs = setup_inputs


def setup_inputs(seed=0):
    import zlib

    import numpy as np

    out = dict(_drawn_inputs(seed))
    spreads = {'L0_gnn_bias': (0.0, 0.1),
     'L0_ffn_router_b1': (0.0, 0.1),
     'L0_ffn_router_b2': (0.0, 0.1),
     'L0_ffn_expert_b1': (0.0, 0.697),
     'L0_ffn_expert_b2': (0.0, 0.295),
     'L0_ffn_expert_b3': (0.0, 0.1)}
    factors = {}
    for name, (base, spread) in spreads.items():
        noise = np.random.default_rng([zlib.crc32(name.encode()), seed]).standard_normal(out[name].shape)
        drawn = base * np.exp(spread * noise) if base else spread * noise
        out[name] = jnp.asarray(drawn.astype(out[name].dtype))
    for name, factor in factors.items():
        out[name] = (out[name] * factor).astype(out[name].dtype)
    return out
```

```python
import concourse.bass as bass
from concourse import mybir
from collections import namedtuple
from contextlib import ExitStack


N, D, H, C = 3125, 256, 4, 64
NW, NP = 25, 125
E_IN = 53125
NT = 18
EC = 128 * NT
BLK = 8
NCOL = 416
NB_P = NCOL // BLK
NB = 128 * NB_P
E_PAD = 128 * NCOL + EC
PAD_DST = 4095
HC = C + 1
ROW = H * HC
K2 = D // 128
EX, RH = 6, 128
BIG = 1.0e30
EPS = 1e-5
SLOPE = 0.2
T_GROUPS = [range(g, min(g + 4, NT)) for g in range(0, NT, 4)]
NG = len(T_GROUPS)
SORT_KEYS = 3328
SORT_CHUNKS = 128 * NCOL // SORT_KEYS

FFN = [("turn", 0), ("hidden", 0), ("l1", 0), ("logits", 0), ("l1", 1), ("l2", 0), ("l1", 2), ("l2", 1),
       ("l1", 3), ("l2", 2), ("l1", 4), ("l2", 3), ("l1", 5), ("l2", 4), ("turn_w", 0), ("l2", 5),
       ("bias3", 0), ("l3", 0), ("l3", 1), ("l3", 2), ("l3", 3), ("l3", 4), ("l3", 5)]
NF = len(FFN)
BY_DVE = ("logits", "bias3", "l3")
N_FD = sum(k in BY_DVE for k, _ in FFN)
N_FA = NF - N_FD
SPREAD_AT = 8

Win = namedtuple("Win", "w q half")


def piece(kind, e=0):
    return FFN.index((kind, e))


def taken(m):
    dve = FFN[m][0] in BY_DVE
    return dve, sum((k in BY_DVE) == dve for k, _ in FFN[:m + 1])


def gat_ffn(nc, x, src, dst, w_gnn, att_src, att_dst, gnn_bias, rw1, rb1, rw2, rb2,
            ew1, eb1, ew2, eb2, ew3, eb3, out):
    f32, i32, u32 = mybir.dt.float32, mybir.dt.int32, mybir.dt.uint32
    ALU, ACT, AX = mybir.AluOpType, mybir.ActivationFunctionType, mybir.AxisListType

    ctx = ExitStack()
    with ctx:
        def sb(name, shape, dt=f32):
            return ctx.enter_context(nc.sbuf_tensor(name, shape, dt))

        def sem(name):
            return ctx.enter_context(nc.semaphore(name))

        table = nc.dram_tensor("table", (N, ROW), f32, kind="Internal").ap()
        edges = nc.dram_tensor("edges", (E_PAD, 2), i32, kind="Internal").ap()

        ident = sb("ident", [128, 128])
        ones = sb("ones", [128, NP])
        scrap = sb("scrap", [1, 1])
        tick = sb("tick", [1, 1])
        iota_n = sb("iota_n", [128, NP])
        wbase = sb("wbase", [128, NW])
        block_up = sb("block_up", [128, NB_P])
        block_down = sb("block_down", [128, NB_P])
        pass_step = sb("pass_step", [NW, NW])
        iota_e = sb("iota_e", [NP, 8])
        wx = sb("wx", [128, K2, ROW + H])
        att = sb("att", [128, 2, H, C])
        att_tmp = sb("att_tmp", [128, H, C])
        gbias = sb("gbias", [NP, D])
        rb2_b = sb("rb2_b", [NP, EX])
        brows = sb("brows", [4 * EX + 1, 128])
        bcols = sb("bcols", [128, 4 * EX + 1])
        b3 = sb("b3", [EX, D])
        r1 = sb("r1", [128, K2, RH])
        r2 = sb("r2", [RH, EX])
        w1 = sb("w1", [128, EX, K2, D])
        w2 = sb("w2", [128, EX, K2, D])
        w3 = sb("w3", [128, EX, K2, D])
        work = sb("work", [128, NT * (128 + ROW)])
        X = work[0:NP, 0:NW * D].rearrange("p (t d) -> p t d", d=D)
        xw = sb("xw", [NP, 2, D])
        HS = sb("HS", [NP, NW, ROW + H])
        EI = sb("EI", [128, 2, NT, 2], i32)
        XEI = sb("XEI", [128, NT, 2], i32)
        G = sb("G", [128, 2, NT, ROW])
        O = sb("O", [128, 2, NT, NP])
        OT = work[0:NP, 0:NT * 128].rearrange("p (j e) -> p j e", e=128)
        MSG = work[:, NT * 128:NT * (128 + ROW)].rearrange("p (j r) -> p j r", r=ROW)

        def pass_tiles(s):
            t = {}
            for name, shape in dict(dstf=[128, NT], same=[128, NT], first=[128, NT], inside=[128, NT],
                                    pen=[128, H, NT], a=[128, H, NT], run=[128, H, NT], fa=[128, H, NT],
                                    cand=[128, H, 2], mid=[128, NT, H + 1],
                                    diag=[128, H, 2, 128]).items():
                t[name] = sb(f"{name}_{s}", shape)
            return t

        MAIN_T, EXTRA_T = pass_tiles("m"), pass_tiles("x")
        penn = sb("penn", [NP, 2, 128])
        masked = sb("masked", [NP, H, 256])
        cmax = sb("cmax", [NP, H])
        cmid = sb("cmid", [NP, 1])
        nmax = sb("nmax", [NP, H])
        nval = sb("nval", [NP, 2, H])
        lold = sb("lold", [NP, H])
        own = sb("own", [NP, H])
        fac = sb("fac", [NP, H])
        al = sb("al", [128, NT, H])
        lr = sb("lr", [128, NT, H])
        ev = sb("ev", [128, NT, H])
        st = sb("st", [NP, ROW])
        rden = sb("rden", [NP, H])
        gat = sb("gat", [NP, D])
        x1 = sb("x1", [NP, D])
        xn = sb("xn", [NP, 2, D])
        stats = sb("stats", [NP, NW, 6])
        mean = sb("mean", [NP, NW])
        rs = sb("rs", [NP, NW])
        rv = sb("rv", [NP, NW])
        rt = sb("rt", [NP, NW])
        mv = sb("mv", [NP, 2])
        xT = sb("xT", [128, 2, K2, NP])
        rhid = sb("rhid", [RH, NP])
        h1 = sb("h1", [128, 2, K2, NP])
        h2 = sb("h2", [128, EX, K2, NP])
        lg = sb("lg", [NP, EX])
        lmx = sb("lmx", [NP, 1])
        pex = sb("pex", [NP, EX])
        psm = sb("psm", [NP, 1])
        prob = sb("prob", [NP, 8])
        top = sb("top", [NP, 8])
        topi = sb("topi", [NP, 8], u32)
        topf = sb("topf", [NP, 2])
        gap = sb("gap", [NP, 1])
        e2 = sb("e2", [NP, 1])
        pw = sb("pw", [NP, 2])
        wa = sb("wa", [NP, 8])
        wb = sb("wb", [NP, 8])
        wT = sb("wT", [8, NP])
        ya = sb("ya", [NP, D])
        yo = sb("yo", [NP, 2, D])
        SQ = E_IN // NP
        pairs_in = G[0:NP, 0, 0:4, :].rearrange("p a b -> p (a b)")[:, 0:2 * SQ].bitcast(i32).rearrange(
            "p (s k) -> p s k", k=2)
        src_in = G[0:NP, 1, 0:4, :].rearrange("p a b -> p (a b)")[:, 0:SQ].bitcast(i32)
        dst_in = G[0:NP, 1, 0:4, :].rearrange("p a b -> p (a b)")[:, SQ:2 * SQ].bitcast(i32)
        n_pad = E_PAD - E_IN
        pads = sb("pads", [3, n_pad // 3, 2], i32)
        pairs = G[:, 0, 4:8, :].rearrange("p a b -> p (a b)")[:, 0:2 * NCOL].bitcast(i32).rearrange(
            "p (s k) -> p s k", k=2)
        bmin = sb("bmin", [128, NB_P])
        bmax = sb("bmax", [128, NB_P])
        hits = MSG[:, 0:5, :].rearrange("p a b -> p (a b)").rearrange("p (w b) -> p w b", b=NB_P)
        hits2 = MSG[:, 5:10, :].rearrange("p a b -> p (a b)").rearrange("p (w b) -> p w b", b=NB_P)
        ends = sb("ends", [128, 2, NW])
        wends = sb("wends", [NW, 2])
        wplan = sb("wplan", [NW, 2])
        wtmp = sb("wtmp", [NW, NW])
        plan = sb("plan", [1, 2 * NW + 1], i32)

        PS = ctx.enter_context(nc.psum_tensor("PS", [128, 8, 512], f32))
        p_cand = PS[:, 2:4, :].rearrange("p a b -> p (a b)")
        p_mid = PS[0:NP, 1, 0:H + 1]
        p_spread = PS[:, 4, 8:8 + NT * 2 * H].rearrange("p (j k h) -> p j k h", k=2, h=H)
        p_sum = PS[0:NP, 4, 160:160 + ROW]

        def bank(m):
            return PS[:, 5 + m % 3, :]

        s_const = sem("s_const")
        s_x = sem("s_x")
        s_ein = sem("s_ein")
        s_pairs = sem("s_pairs")
        s_edged = sem("s_edged")
        s_back = sem("s_back")
        s_wg = sem("s_wg")
        s_wb = sem("s_wb")
        s_we = sem("s_we")
        s_chain = sem("s_chain")
        s_tick = sem("s_tick")
        s_stats = sem("s_stats")
        s_wx = sem("s_wx")
        s_ends = sem("s_ends")
        s_endt = sem("s_endt")
        s_wplan = sem("s_wplan")
        s_plant = sem("s_plant")
        s_plan = sem("s_plan")
        s_bct = sem("s_bct")
        s_bc = sem("s_bc")
        s_xn0 = sem("s_xn0")
        s_xt0 = sem("s_xt0")
        s_xe0 = sem("s_xe0")
        s_h0 = sem("s_h0")
        s_hs = sem("s_hs")
        s_table = sem("s_table")
        s_load = [sem("s_load0"), sem("s_load1")]
        s_xw = [sem("s_xw0"), sem("s_xw1")]
        s_gath = [sem("s_gath0"), sem("s_gath1")]
        s_out = [sem("s_out0"), sem("s_out1")]
        s_x1 = sem("s_x1")
        s_piece = sem("s_piece")
        s_fa = sem("s_fa")
        s_fd = sem("s_fd")
        s_lgm = sem("s_lgm")
        s_pex = sem("s_pex")
        s_gap = sem("s_gap")
        s_e2 = sem("s_e2")
        s_wts = sem("s_wts")

        Sems = namedtuple("Sems", "onehot turned ot cand cands nval spread fac zed ev den msg agg merged")

        def pass_sems(s):
            return Sems(*[sem(f"s_{n}_{s}") for n in Sems._fields])

        MAIN_S, EXTRA_S = pass_sems("m"), pass_sems("x")
        s_xload = sem("s_xload")
        s_xgath = sem("s_xgath")

        block = ctx.enter_context(nc.Block())

        def row(t, w):
            return t[:, bass.ds(w, 1), :].rearrange("p a d -> p (a d)")

        def most_passes(eng):
            eng.wait_ge(s_plan, 1)
            return eng.value_load(plan[0:1, 2 * NW:2 * NW + 1], min_val=1, max_val=NW)

        def extras(eng, most, x, w, body):
            with eng.If(most > 1):
                n = eng.value_load(plan[0:1, bass.ds(NW + w, 1)], min_val=1, max_val=NW)
                with eng.If(n > 1):
                    with eng.Fori(1, n) as c:
                        body(eng.snap(x), c)
                        eng.reg_add(x, x, 1)

        def windows(body):
            def run(eng):
                body(Win(0, 0, 0), False, True, True)
                with eng.Fori(0, (NW - 3) // 2) as i:
                    body(Win(i * 2 + 1, 1, i), True, True, True)
                    body(Win(i * 2 + 2, 0, i + 1), True, True, True)
                body(Win(NW - 2, 1, (NW - 2) // 2), True, True, False)
                body(Win(NW - 1, 0, (NW - 1) // 2), True, False, False)
            return run

        def val(eng, v):
            return v if isinstance(v, int) else eng.to_reg(v)

        def counter(eng, name):
            x = eng.alloc_register(name)
            eng.reg_mov(x, 0)
            return x

        @block.sync
        def _(sp):
            sp.dma_start(src_in, src.rearrange("(p s) -> p s", p=NP)).then_inc(s_ein, 16)
            sp.dma_start(dst_in, dst.rearrange("(p s) -> p s", p=NP)).then_inc(s_ein, 16)
            xv = x.rearrange("(t p) d -> p t d", p=NP)
            for a, b in ((0, 112), (112, NP)):
                sp.dma_start(X[a:b, :, :], xv[a:b, :, :]).then_inc(s_x, 16)
            sp.wait_ge(s_pairs, 2)
            sp.wait_ge(s_const, 2)
            sp.dma_start(edges[0:E_IN, :].rearrange("(p s) k -> p (s k)", p=NP),
                         pairs_in.rearrange("p s k -> p (s k)")).then_inc(s_edged, 16)
            sp.dma_start(edges[E_IN:E_PAD, :].rearrange("(p s) k -> p (s k)", p=3),
                         pads[:, :, :].rearrange("p s k -> p (s k)")).then_inc(s_edged, 16)
            sp.wait_ge(s_edged, 32)
            sp.dma_start(pairs.rearrange("p s k -> p (s k)"),
                         edges[0:128 * NCOL, :].rearrange("(p s) k -> p (s k)", p=128)).then_inc(s_back, 16)
            tv = table.rearrange("(t p) r -> p t r", p=NP)
            for c in range(5):
                sp.wait_ge(s_hs, 5 * (c + 1))
                for a, b in ((0, 112), (112, NP)):
                    sp.dma_start(tv[a:b, 5 * c:5 * c + 5, :],
                                 HS[a:b, 5 * c:5 * c + 5, 0:ROW]).then_inc(s_table, 16)

            edge_list = edges.rearrange("e k -> (e k)")
            x_list, out_list = x.rearrange("n d -> (n d)"), out.rearrange("n d -> (n d)")
            most = most_passes(sp)
            x_no = counter(sp, "x_sp")

            def first_edge(w):
                return offset(sp.value_load(plan[0:1, bass.ds(w, 1)], min_val=0, max_val=2 * BLK * NB))

            def offset(v):
                val(sp, v * 4)
                return v

            def load(e0, q):
                sp.dma_start(EI[:, q, :, :].rearrange("p j k -> p (j k)"),
                             edge_list[bass.ds(e0, 2 * EC)].rearrange("(p j) -> p j", p=128))\
                    .then_inc(s_load[q], 16)

            def window(v, prev, nxt, nxt2):
                if nxt2:
                    gathered, seen = val(sp, 16 * NT * (v.half + 1)), val(sp, v.w + 1)
                    e0 = first_edge(v.w + 2)
                    sp.wait_ge(s_gath[v.q], gathered)
                    sp.wait_ge(MAIN_S.onehot, seen)
                    load(e0, v.q)

                def extra(n, c):
                    e0 = first_edge(v.w)
                    start = nc.s_assert_within(e0 + c * (2 * EC), 0, 2 * BLK * NB, skip_runtime_bounds_check_because=
                                               "a pass starts before the window's last edge")
                    start, main, before = offset(start), val(sp, v.w + 1), val(sp, n + 1)
                    sp.wait_ge(MAIN_S.merged, main)
                    sp.wait_ge(EXTRA_S.merged, before)
                    sp.dma_start(XEI[:, :, :].rearrange("p j k -> p (j k)"),
                                 edge_list[bass.ds(start, 2 * EC)].rearrange("(p j) -> p j", p=128))\
                        .then_inc(s_xload, 16)

                extras(sp, most, x_no, v.w, extra)
                if nxt:
                    if prev:
                        used = val(sp, v.w)
                    at = offset((v.w + 1) * (NP * D))
                    if prev:
                        sp.wait_ge(s_x1, used)
                    load_x(at, 1 - v.q)
                if prev:
                    store(v.w - 1, 1 - v.q)

            def store(w, q):
                done, at = val(sp, (w + 1) * N_FD), offset(w * (NP * D))
                sp.wait_ge(s_fd, done)
                sp.dma_start(out_list[bass.ds(at, NP * D)].rearrange("(p d) -> p d", p=NP), yo[:, q, :]).then_inc(s_out[q], 16)

            def load_x(at, q):
                sp.dma_start(xw[:, q, :], x_list[bass.ds(at, NP * D)].rearrange("(p d) -> p d", p=NP)).then_inc(s_xw[q], 16)

            load(first_edge(0), 0)
            load(first_edge(1), 1)
            load_x(0, 0)
            windows(window)(sp)
            store(NW - 1, (NW - 1) % 2)
            sp.wait_ge(s_out[0], 16 * ((NW + 1) // 2))
            sp.wait_ge(s_out[1], 16 * (NW // 2))
            sp.wait_ge(s_table, 160)

        @block.gpsimd
        def _(pool):
            pool.memset(pads[:, :, 0:1], 0).then_inc(s_const, 1)
            pool.memset(pads[:, :, 1:2], PAD_DST).then_inc(s_const, 1)
            pool.memset(ident[:, :], 0.0).then_inc(s_const, 1)
            pool.wait_ge(s_const, 3)
            pool.affine_select(out=ident[:, :], in_=ident[:, :], compare_op=ALU.not_equal, fill=1.0, base=0,
                               pattern=[[-1, 128]], channel_multiplier=1).then_inc(s_const, 1)
            pool.memset(tick[:, :], 0.0).then_inc(s_const, 1)
            pool.memset(ones[:, :], 1.0).then_inc(s_const, 1)

            def hold():
                pool.tensor_tensor(tick[:, :], tick[:, :], tick[:, :], ALU.mult).then_inc(s_tick, 1)
                pool.wait_ge(s_tick, 1)
                pool.sem_clear(s_tick)

            def count(t, step, n, base=0, mult=0):
                pool.iota(t, pattern=[[step, n]], base=base, channel_multiplier=mult,
                          allow_small_or_imprecise_dtypes=True).then_inc(s_const, 1)

            count(iota_n[:, :], 1, NP)
            count(wbase[:, :], NP, NW)
            count(block_up[:, :], 1, NB_P, base=1, mult=NB_P)
            count(block_down[:, :], -1, NB_P, base=NB, mult=-NB_P)
            count(pass_step[:, :], EC // BLK, NW)
            count(iota_e[:, :], 1, 8)

            pool.wait_ge(s_const, 12)
            most = most_passes(pool)
            x_no = counter(pool, "x_pool")
            pool.wait_ge(s_table, 160)

            def gather(idx, q, done):
                for j in range(NT):
                    pool.indirect_dma_start(
                        G[:, q, j, :], None, table,
                        bass.IndirectOffsetOnAxis(ap=idx[:, j, 0:1], axis=0)).then_inc(done, 16)

            def window(v, prev, nxt, nxt2):
                if nxt:
                    loaded, used = val(pool, 16 * (v.half + v.q + 1)), val(pool, v.w)
                    pool.wait_ge(s_load[1 - v.q], loaded)
                    hold()
                    if prev:
                        pool.wait_ge(MAIN_S.msg, used)
                        hold()
                    gather(EI[:, 1 - v.q, :, :], 1 - v.q, s_gath[1 - v.q])

                def extra(n, c):
                    pool.wait_ge(s_xload, (n + 1) * 16)
                    hold()
                    gather(XEI, v.q, s_xgath)

                extras(pool, most, x_no, v.w, extra)

            pool.wait_ge(s_load[0], 16)
            gather(EI[:, 0, :, :], 0, s_gath[0])
            windows(window)(pool)

        @block.vector
        def _(dve):
            v_ = nc.vector
            links = [0]

            def link(ins):
                links[0] += 1
                ins.then_inc(s_chain, 1)
                dve.wait_ge(s_chain, links[0])

            def tell(ins, done, n):
                ins.then_inc(done, 1)
                dve.wait_ge(done, n)

            def settle():
                link(v_.memset(scrap[:, :], 0.0))
                relink()

            def relink():
                dve.sem_clear(s_chain)
                links[0] = 0

            def rsqrt(r, var, v, t):
                link(v_.tensor_scalar(v, var, EPS, None, ALU.add))
                link(v_.tensor_scalar(r.bitcast(i32), v.bitcast(i32), -0.5, 1597463007.0, ALU.mult, ALU.add))
                for _ in range(4):
                    link(v_.tensor_tensor(t, v, r, ALU.mult))
                    link(v_.tensor_tensor(t, t, r, ALU.mult))
                    link(v_.tensor_scalar(t, t, -0.5, 1.5, ALU.mult, ALU.add))
                    link(v_.tensor_tensor(r, r, t, ALU.mult))

            dve.wait_ge(s_ein, 32)
            tell(v_.tensor_copy(pairs_in[:, :, 0], src_in), s_pairs, 1)
            tell(v_.tensor_copy(pairs_in[:, :, 1], dst_in), s_pairs, 2)
            for t in (MAIN_T, EXTRA_T):
                link(v_.memset(t["same"][:, 0:1], 0.0))
                link(v_.memset(t["first"][:, 0:1], 1.0))
                link(v_.memset(t["inside"][:, NT - 1:NT], 0.0))
            tell(v_.memset(prob[:, EX:8], -1.0), EXTRA_S.merged, 1)

            dve.wait_ge(s_wg, 64)
            for k in range(K2):
                wk = wx[:, k, 0:ROW].rearrange("p (h c) -> p h c", c=HC)
                for a in range(2):
                    link(v_.tensor_tensor(att_tmp[:, :, :], wk[:, :, 0:C], att[:, a, :, :], ALU.mult))
                    to = wk[:, :, C:HC].rearrange("p h c -> p (h c)") if a == 0 else wx[:, k, ROW:ROW + H]
                    tell(v_.tensor_reduce(to, att_tmp[:, :, :], AX.X, ALU.add), s_wx, 2 * k + a + 1)

            dve.wait_ge(s_x, 32)
            with dve.Fori(0, NW) as t:
                v_.bn_stats(row(stats, t), row(X, t)).then_inc(s_stats, 1)
            dve.wait_ge(s_stats, NW)
            link(v_.tensor_tensor(mean[:, :], stats[:, :, 1], stats[:, :, 4], ALU.add))
            link(v_.tensor_tensor(rt[:, :], stats[:, :, 1], stats[:, :, 4], ALU.subtract))
            link(v_.tensor_tensor(rt[:, :], rt[:, :], rt[:, :], ALU.mult))
            link(v_.tensor_tensor(rv[:, :], stats[:, :, 2], stats[:, :, 5], ALU.add))
            link(v_.scalar_tensor_tensor(rv[:, :], rt[:, :], float(D // 4), rv[:, :], ALU.mult, ALU.add))
            link(v_.tensor_scalar(rv[:, :], rv[:, :], 1.0 / D, None, ALU.mult))
            link(v_.tensor_scalar(mean[:, :], mean[:, :], 0.5, None, ALU.mult))
            rsqrt(rs[:, :], rv[:, :], rv[:, :], rt[:, :])
            relink()

            def normalise(t, q):
                tell(v_.tensor_scalar(xn[:, q, :], row(X, t), mean[:, bass.ds(t, 1)], rs[:, bass.ds(t, 1)],
                                 ALU.subtract, ALU.mult), s_xn0, t + 1)

            def keep_h(t, q):
                dve.wait_ge(s_h0, t + 1)
                tell(v_.tensor_copy(row(HS, t), PS[0:NP, 2 + q, 0:ROW + H]), s_hs, t + 1)

            normalise(0, 0)
            normalise(1, 1)
            with dve.Fori(0, (NW - 3) // 2) as i:
                for q in range(2):
                    dve.wait_ge(s_xt0, i * 2 + q + 1)
                    normalise(i * 2 + q + 2, q)
                    keep_h(i * 2 + q, q)
                settle()
            dve.wait_ge(s_xt0, NW - 2)
            normalise(NW - 1, 0)
            for t in range(NW - 3, NW):
                keep_h(t, t % 2)

            dve.wait_ge(s_back, 16)
            dv = pairs[:, :, 1].rearrange("p (b k) -> p b k", k=BLK)
            link(v_.tensor_reduce(bmin[:, :], dv, AX.X, ALU.min))
            link(v_.tensor_reduce(bmax[:, :], dv, AX.X, ALU.max))
            dve.wait_ge(s_const, 12)
            shape = [128, NW, NB_P]

            def over_w(t):
                return t[:, :].unsqueeze(1).broadcast_to(shape)

            def over_b(t):
                return t[:, :].unsqueeze(2).broadcast_to(shape)

            link(v_.tensor_tensor(hits2, over_w(bmax), over_b(wbase), ALU.is_ge))
            link(v_.tensor_scalar(bmin[:, :], bmin[:, :], float(NP - 1), None, ALU.subtract))
            link(v_.tensor_tensor(hits, over_w(bmin), over_b(wbase), ALU.is_le))
            link(v_.tensor_tensor(hits, hits, hits2, ALU.mult))
            link(v_.tensor_tensor(hits2, hits, over_w(block_up), ALU.mult))
            link(v_.tensor_reduce(ends[:, 0, :], hits2, AX.X, ALU.max))
            link(v_.tensor_tensor(hits2, hits, over_w(block_down), ALU.mult))
            tell(v_.tensor_reduce(ends[:, 1, :], hits2, AX.X, ALU.max), s_ends, 1)
            dve.wait_ge(s_endt, 1)
            link(v_.tensor_reduce(wends[:, :], PS[0:NW, 4, 0:256].rearrange("p (k c) -> p k c", k=2), AX.X,
                                  ALU.max))
            link(v_.tensor_scalar(wplan[:, 0:1], wends[:, 1:2], -1.0, float(NB), ALU.mult, ALU.add))
            link(v_.tensor_tensor(wends[:, 0:1], wends[:, 0:1], wplan[:, 0:1], ALU.subtract))
            link(v_.tensor_scalar(wtmp[:, :], pass_step[:, :], wends[:, 0:1], None, ALU.is_lt))
            link(v_.tensor_reduce(wplan[:, 1:2], wtmp[:, :], AX.X, ALU.add))
            link(v_.tensor_scalar(wplan[:, 1:2], wplan[:, 1:2], 1.0, None, ALU.max))
            tell(v_.tensor_scalar(wplan[:, 0:1], wplan[:, 0:1], float(2 * BLK), None, ALU.mult), s_wplan, 1)
            dve.wait_ge(s_plant, 1)
            link(v_.tensor_copy(plan[0:1, 0:2 * NW], PS[0:1, 4, 256:256 + 2 * NW]))
            link(v_.tensor_reduce(wtmp[0:1, 0:1], PS[0:1, 4, 256 + NW:256 + 2 * NW], AX.X, ALU.max))
            relink()
            tell(v_.tensor_copy(plan[0:1, 2 * NW:2 * NW + 1], wtmp[0:1, 0:1]), s_plan, 1)

            most = most_passes(dve)
            x_no = counter(dve, "x_dve")

            def edges_of(t, ei, o, w, n, S):
                link(v_.tensor_scalar(t["dstf"][:, :], ei[:, :, 1], wbase[:, bass.ds(w, 1)], None, ALU.subtract))
                tell(v_.tensor_tensor(o, iota_n[:, :].unsqueeze(1).broadcast_to([128, NT, NP]),
                                 t["dstf"][:, :].unsqueeze(2).broadcast_to([128, NT, NP]),
                                 ALU.is_equal), S.onehot, n + 1)
                link(v_.tensor_tensor(t["same"][:, 1:NT], t["dstf"][:, 1:NT], t["dstf"][:, 0:NT - 1],
                                      ALU.is_equal))
                link(v_.tensor_scalar(t["pen"][:, :, :], t["same"][:, :].unsqueeze(1).broadcast_to([128, H, NT]),
                                 -1.0, BIG, ALU.add, ALU.mult))
                link(v_.tensor_tensor_scan(t["first"][:, 1:NT], t["same"][:, 1:NT], t["same"][:, 1:NT], 1.0,
                                           ALU.mult, ALU.mult))
                link(v_.tensor_scalar(t["inside"][:, 0:NT - 1], t["first"][:, 0:NT - 1], -1.0, None, ALU.add))
                link(v_.scalar_tensor_tensor(t["inside"][:, 0:NT - 1], t["same"][:, 1:NT], -1.0,
                                             t["inside"][:, 0:NT - 1], ALU.add, ALU.mult))

            def candidates(t, g, n, S):
                gv = g.rearrange("p j (h c) -> p h j c", c=HC)[:, :, :, C]
                link(v_.tensor_copy(t["a"][:, :, :], gv))
                flat = "p h j -> p (h j)"
                link(v_.tensor_tensor_scan(t["run"][:, :, :].rearrange(flat), t["pen"][:, :, :].rearrange(flat),
                                           t["a"][:, :, :].rearrange(flat), -BIG, ALU.add, ALU.max))
                link(v_.tensor_scalar(t["fa"][:, :, :],
                                      t["first"][:, :].unsqueeze(1).broadcast_to([128, H, NT]),
                                      -1.0, BIG, ALU.add, ALU.mult))
                link(v_.tensor_tensor(t["fa"][:, :, :], t["fa"][:, :, :], t["a"][:, :, :], ALU.add))
                link(v_.tensor_copy(t["cand"][:, :, 1], t["run"][:, :, NT - 1]))
                link(v_.tensor_reduce(t["cand"][:, :, 0], t["fa"][:, :, :], AX.X, ALU.max))
                link(v_.tensor_tensor(t["mid"][:, :, 0:H], t["run"][:, :, :].rearrange("p h j -> p j h"),
                                 t["inside"][:, :].unsqueeze(2).broadcast_to([128, NT, H]), ALU.mult))
                link(v_.tensor_copy(t["mid"][:, :, H], t["inside"][:, :]))
                shape = [128, 2 * H, 128]
                tell(v_.tensor_tensor(t["diag"][:, :, :, :].rearrange("p h k e -> p (h k) e"),
                                 ident[:, :].unsqueeze(1).broadcast_to(shape),
                                 t["cand"][:, :, :].rearrange("p h k -> p (h k)").unsqueeze(2)
                                 .broadcast_to(shape), ALU.mult), S.cand, n + 1)

            def maxima(t, w, n, first, S):
                dve.wait_ge(S.ot, (n + 1) * NG)
                ends_of = OT[:, 0:NT:NT - 1, :]
                link(v_.tensor_scalar(penn[:, :, :], ends_of, -1.0, BIG, ALU.add, ALU.mult))
                dve.wait_ge(S.cands, n + 1)
                shape = [NP, H, 256]
                link(v_.tensor_tensor(masked[:, :, :], p_cand[0:NP, :].rearrange("p (h e) -> p h e", h=H),
                                      penn[:, :, :].rearrange("p k e -> p (k e)").unsqueeze(1)
                                      .broadcast_to(shape), ALU.add))
                link(v_.tensor_reduce(cmax[:, :], masked[:, :, :], AX.X, ALU.max))
                link(v_.tensor_scalar(cmid[:, :], p_mid[:, H:H + 1], -1.0, BIG, ALU.add, ALU.mult))
                link(v_.scalar_tensor_tensor(cmax[:, :], p_mid[:, 0:H], cmid[:, :], cmax[:, :],
                                             ALU.add, ALU.max))
                hs = row(HS, w)
                a_dst = hs[:, ROW:ROW + H]
                if first:
                    old = hs[:, 0:ROW].rearrange("p (h c) -> p h c", c=HC)[:, :, C]
                    link(v_.tensor_tensor(own[:, :], old, a_dst, ALU.add))
                    link(v_.scalar_tensor_tensor(lold[:, :], own[:, :], SLOPE, own[:, :], ALU.mult, ALU.max))
                    link(v_.tensor_tensor(nmax[:, :], cmax[:, :], old, ALU.max))
                else:
                    link(v_.tensor_copy(lold[:, :], nval[:, 1, :]))
                    link(v_.tensor_tensor(nmax[:, :], cmax[:, :], nmax[:, :], ALU.max))
                link(v_.tensor_tensor(cmax[:, :], nmax[:, :], a_dst, ALU.add))
                link(v_.tensor_copy(nval[:, 0, :], a_dst))
                link(v_.scalar_tensor_tensor(nval[:, 1, :], cmax[:, :], SLOPE, cmax[:, :], ALU.mult, ALU.max))
                tell(v_.tensor_tensor(lold[:, :], lold[:, :], nval[:, 1, :], ALU.subtract), S.nval, n + 1)

            def exponents(t, n, S):
                dve.wait_ge(S.spread, n + 1)
                link(v_.tensor_tensor(al[:, :, :], t["a"][:, :, :].rearrange("p h j -> p j h"),
                                      p_spread[:, :, 0, :], ALU.add))
                link(v_.scalar_tensor_tensor(lr[:, :, :], al[:, :, :], SLOPE, al[:, :, :], ALU.mult, ALU.max))
                link(v_.tensor_tensor(lr[:, :, :], lr[:, :, :], p_spread[:, :, 1, :], ALU.subtract))
                tell(v_.tensor_scalar(lr[:, :, :], lr[:, :, :], 0.0, None, ALU.min), S.zed, n + 1)

            def messages(g, n, S):
                dve.wait_ge(S.ev, n + 1)
                tell(v_.tensor_tensor(MSG[:, :, :].rearrange("p j (h c) -> p (j h) c", c=HC)[:, :, 0:C],
                                 g.rearrange("p j (h c) -> p (j h) c", c=HC)[:, :, 0:C],
                                 ev[:, :, :].rearrange("p j h -> p (j h)").unsqueeze(2)
                                 .broadcast_to([128, NT * H, C]), ALU.mult), S.msg, n + 1)

            def merge(w, n, first, S):
                dve.wait_ge(S.fac, n + 1)
                s3 = st[:, :].rearrange("p (h c) -> p h c", c=HC)
                old = row(HS, w)[:, 0:ROW].rearrange("p (h c) -> p h c", c=HC) if first else s3
                link(v_.tensor_tensor(s3, old, fac[:, :].unsqueeze(2).broadcast_to([NP, H, HC]), ALU.mult))
                if first:
                    link(v_.tensor_copy(s3[:, :, C], fac[:, :]))
                relink()
                dve.wait_ge(S.agg, n + 1)
                v_.tensor_tensor(st[:, :], st[:, :], p_sum, ALU.add).then_inc(S.merged, 1)
                if not first:
                    dve.wait_ge(S.merged, n + 2)
                    settle()

            def finish(w, q, half):
                dve.wait_ge(MAIN_S.merged, w + 1)
                s3 = st[:, :].rearrange("p (h c) -> p h c", c=HC)
                link(v_.tensor_scalar(rden[:, :], s3[:, :, C], 1e-16, None, ALU.add))
                link(v_.reciprocal(rden[:, :], rden[:, :]))
                link(v_.tensor_tensor(gat[:, :].rearrange("p (h c) -> p h c", c=C), s3[:, :, 0:C],
                                      rden[:, :].unsqueeze(2).broadcast_to([NP, H, C]), ALU.mult))
                link(v_.tensor_tensor(gat[:, :], gat[:, :], gbias[:, :], ALU.add))
                dve.wait_ge(s_xw[q], 16 * (half + 1))
                link(v_.scalar_tensor_tensor(x1[:, :], gat[:, :], 0.0, xw[:, q, :], ALU.max, ALU.add))
                link(v_.bn_stats(stats[:, 0, :], x1[:, :]))
                link(v_.bn_aggr(mv[:, :], stats[:, 0, :]))
                rsqrt(rs[:, 0:1], mv[:, 1:2], rv[:, 0:1], rt[:, 0:1])
                relink()
                v_.tensor_scalar(xn[:, 0, :], x1[:, :], mv[:, 0:1], rs[:, 0:1],
                                 ALU.subtract, ALU.mult).then_inc(s_x1, 1)

            def take(u, m):
                dve.wait_ge(s_piece, u * NF + m + 1)

            def route(u):
                m = piece("logits")
                take(u, m)
                tell(v_.tensor_tensor(lg[:, :], bank(m)[0:NP, 0:EX], rb2_b[:, :], ALU.add), s_fd, u * N_FD + 1)
                link(v_.tensor_reduce(lmx[:, :], lg[:, :], AX.X, ALU.max))
                tell(v_.tensor_scalar(lg[:, :], lg[:, :], lmx[:, :], None, ALU.subtract), s_lgm, u + 1)
                dve.wait_ge(s_pex, u + 1)
                link(v_.tensor_reduce(psm[:, :], pex[:, :], AX.X, ALU.add))
                link(v_.reciprocal(psm[:, :], psm[:, :]))
                link(v_.tensor_scalar(prob[:, 0:EX], pex[:, :], psm[:, :], None, ALU.mult))
                link(v_.max(top[:, :], prob[:, :]))
                link(v_.max_index(topi[:, :], top[:, :], prob[:, :]))
                tell(v_.tensor_tensor(gap[:, :], top[:, 1:2], top[:, 0:1], ALU.subtract), s_gap, u + 1)
                link(v_.tensor_copy(topf[:, :], topi[:, 0:2]))
                dve.wait_ge(s_e2, u + 1)
                link(v_.tensor_scalar(pw[:, 0:1], e2[:, :], 1.0, None, ALU.add))
                link(v_.reciprocal(pw[:, 0:1], pw[:, 0:1]))
                link(v_.tensor_tensor(pw[:, 1:2], e2[:, :], pw[:, 0:1], ALU.mult))
                link(v_.tensor_scalar(wa[:, :], iota_e[:, :], topf[:, 0:1], pw[:, 0:1], ALU.is_equal, ALU.mult))
                link(v_.tensor_scalar(wb[:, :], iota_e[:, :], topf[:, 1:2], pw[:, 1:2], ALU.is_equal, ALU.mult))
                tell(v_.tensor_tensor(wa[:, :], wa[:, :], wb[:, :], ALU.add), s_wts, u + 1)

            def combine(u, q, half):
                m = piece("bias3")
                take(u, m)
                tell(v_.tensor_tensor(ya[:, :], bank(m)[0:NP, 0:D], x1[:, :], ALU.add), s_fd, u * N_FD + taken(m)[1])
                for e in range(EX):
                    m = piece("l3", e)
                    take(u, m)
                    last = e == EX - 1
                    if last and half is not None:
                        dve.wait_ge(s_out[q], 16 * half)
                    tell(v_.scalar_tensor_tensor(yo[:, q, :] if last else ya[:, :], bank(m)[0:NP, 0:D],
                                            wa[:, e:e + 1], ya[:, :], ALU.mult, ALU.add), s_fd, u * N_FD + taken(m)[1])

            def window(v, prev, nxt, nxt2, tail=False):
                w, q = v.w, v.q
                S, T = MAIN_S, MAIN_T
                if prev:
                    dve.wait_ge(s_x1, w)
                maxima(T, w, w, True, S)
                if prev:
                    route(w - 1)
                exponents(T, w, S)
                messages(G[:, q, :, :], w, S)
                if prev:
                    first_use = isinstance(v.half, int) and (w - 1) < 2
                    combine(w - 1, 1 - q, None if first_use else prev_half(v))
                if nxt:
                    start(Win(w + 1, 1 - q, v.half + q))
                merge(w, w, True, S)

                def extra(n, c):
                    dve.wait_ge(s_xload, (n + 1) * 16)
                    edges_of(EXTRA_T, XEI, O[:, q, :, :], w, n, EXTRA_S)
                    dve.wait_ge(s_xgath, (n + 1) * (16 * NT))
                    candidates(EXTRA_T, G[:, q, :, :], n, EXTRA_S)
                    maxima(EXTRA_T, w, n, False, EXTRA_S)
                    exponents(EXTRA_T, n, EXTRA_S)
                    messages(G[:, q, :, :], n, EXTRA_S)
                    merge(w, n, False, EXTRA_S)

                extras(dve, most, x_no, w, extra)
                finish(w, q, v.half)

            def prev_half(v):
                return v.half if v.q else v.half - 1

            def start(v):
                dve.wait_ge(s_load[v.q], 16 * (v.half + 1))
                edges_of(MAIN_T, EI[:, v.q, :, :], O[:, v.q, :, :], v.w, v.w, MAIN_S)
                dve.wait_ge(s_gath[v.q], 16 * NT * (v.half + 1))
                candidates(MAIN_T, G[:, v.q, :, :], v.w, MAIN_S)

            dve.wait_ge(s_wb, 16 * 7)
            start(Win(0, 0, 0))
            body = window
            body(Win(0, 0, 0), False, True, True)
            body(Win(1, 1, 0), True, True, True)
            body(Win(2, 0, 1), True, True, True)
            with dve.Fori(1, (NW - 3) // 2) as i:
                body(Win(i * 2 + 1, 1, i), True, True, True)
                body(Win(i * 2 + 2, 0, i + 1), True, True, True)
            body(Win(NW - 2, 1, (NW - 2) // 2), True, True, False)
            body(Win(NW - 1, 0, (NW - 1) // 2), True, False, False)
            route(NW - 1)
            combine(NW - 1, (NW - 1) % 2, (NW - 1) // 2)

        @block.scalar
        def _(act):
            def copy(o, i):
                return nc.scalar.activation(o, i, ACT.Copy)

            for k in range(K2):
                act.dma_start(wx[:, k, 0:ROW].rearrange("p (h c) -> p h c", c=HC)[:, :, 0:C],
                              w_gnn[128 * k:128 * k + 128, :].rearrange("p (h c) -> p h c", c=C))\
                    .then_inc(s_wg, 16)
            for a, v in enumerate((att_src, att_dst)):
                act.dma_start(att[:, a, :, :].rearrange("p h c -> p (h c)"),
                              v.rearrange("h c -> (h c)").partition_broadcast(128)).then_inc(s_wg, 16)
            act.dma_start(brows[0:2 * EX, :], eb1.rearrange("e (k p) -> (e k) p", p=128)).then_inc(s_wb, 16)
            act.dma_start(brows[2 * EX:4 * EX, :], eb2.rearrange("e (k p) -> (e k) p", p=128))\
                .then_inc(s_wb, 16)
            act.dma_start(brows[4 * EX:4 * EX + 1, :], rb1.unsqueeze(0)).then_inc(s_wb, 16)
            act.dma_start(gbias[:, :], gnn_bias.partition_broadcast(NP)).then_inc(s_wb, 16)
            act.dma_start(rb2_b[:, :], rb2.partition_broadcast(NP)).then_inc(s_wb, 16)
            act.dma_start(b3[:, :], eb3).then_inc(s_wb, 16)
            act.dma_start(r1[:, :, :], rw1.rearrange("(k p) f -> p k f", p=128)).then_inc(s_wb, 16)
            act.dma_start(r2[:, :], rw2).then_inc(s_we, 16)
            for t, v in ((w1, ew1), (w2, ew2), (w3, ew3)):
                act.dma_start(t[:, :, :, :].rearrange("p e k f -> p (e k) f"),
                              v.rearrange("e (k p) f -> p (e k) f", p=128)).then_inc(s_we, 16)

            act.wait_ge(s_bct, 1)
            copy(bcols[:, :], bank(0)[:, 0:4 * EX + 1]).then_inc(s_bc, 1)

            def evacuate(t, q):
                act.wait_ge(s_xt0, t + 1)
                copy(xT[:, q, :, :].rearrange("p k n -> p (k n)"), PS[:, q, 0:K2 * NP]).then_inc(s_xe0, 1)

            evacuate(0, 0)
            with act.Fori(0, (NW - 1) // 2) as i:
                evacuate(i * 2 + 1, 1)
                evacuate(i * 2 + 2, 0)
            most = most_passes(act)
            x_no = counter(act, "x_act")
            act.wait_ge(s_bc, 1)

            def transposed(n, S):
                for g, cols in enumerate(T_GROUPS):
                    act.wait_ge(S.turned, n * NG + g + 1)
                    copy(OT[:, cols[0]:cols[-1] + 1, :].rearrange("p j e -> p (j e)"),
                         PS[0:NP, g % 2, 0:128 * len(cols)]).then_inc(S.ot, 1)

            def factor(n, S):
                act.wait_ge(S.nval, n + 1)
                nc.scalar.activation(fac[:, :], lold[:, :], ACT.Exp).then_inc(S.fac, 1)

            def exponentials(n, S):
                act.wait_ge(S.zed, n + 1)
                nc.scalar.activation(ev[:, :, :], lr[:, :, :], ACT.Exp).then_inc(S.ev, 1)
                act.wait_ge(S.ev, n + 1)
                copy(MSG[:, :, :].rearrange("p j (h c) -> p j h c", c=HC)[:, :, :, C],
                     ev[:, :, :]).then_inc(S.den, 1)

            def take(u, m):
                kind, e = FFN[m]
                act.wait_ge(s_piece, u * NF + m + 1)
                if kind == "turn":
                    ins = copy(xT[:, 0, :, :].rearrange("p k n -> p (k n)"), bank(m)[:, 0:K2 * NP])
                elif kind == "hidden":
                    ins = nc.scalar.activation(rhid[:, :], bank(m)[:, 0:NP], ACT.Relu,
                                               bias=bcols[:, 4 * EX:4 * EX + 1])
                elif kind == "turn_w":
                    ins = copy(wT[:, :], bank(m)[0:8, 0:NP])
                else:
                    for f in range(K2):
                        to = h1[:, e % 2, f, :] if kind == "l1" else h2[:, e, f, :]
                        col = (2 * EX if kind == "l2" else 0) + 2 * e + f
                        ins = nc.scalar.activation(to, bank(m)[:, f * NP:(f + 1) * NP], ACT.Relu,
                                                   bias=bcols[:, col:col + 1])
                ins.then_inc(s_fa, 1)

            def takes(u, a, b):
                for m in range(a, b):
                    if not taken(m)[0]:
                        take(u, m)
                    if FFN[m] == ("l1", 1):
                        act.wait_ge(s_lgm, u + 1)
                        nc.scalar.activation(pex[:, :], lg[:, :], ACT.Exp).then_inc(s_pex, 1)
                    if FFN[m] == ("l2", 1):
                        act.wait_ge(s_gap, u + 1)
                        nc.scalar.activation(e2[:, :], gap[:, :], ACT.Exp).then_inc(s_e2, 1)

            def window(v, prev, nxt, nxt2):
                w = v.w
                transposed(w, MAIN_S)
                if prev:
                    takes(w - 1, 0, SPREAD_AT)
                factor(w, MAIN_S)
                if prev:
                    takes(w - 1, SPREAD_AT, SPREAD_AT + 1)
                exponentials(w, MAIN_S)
                if prev:
                    takes(w - 1, SPREAD_AT + 1, NF)

                def extra(n, c):
                    transposed(n, EXTRA_S)
                    factor(n, EXTRA_S)
                    exponentials(n, EXTRA_S)

                extras(act, most, x_no, w, extra)

            windows(window)(act)
            takes(NW - 1, 0, NF)

        @block.tensor
        def _(pe):
            mm = nc.tensor.matmul
            pe.wait_ge(s_const, 12)
            pe.wait_ge(s_wb, 16 * 7)
            nc.tensor.transpose(bank(0)[:, 0:4 * EX + 1], brows[:, :], ident[0:4 * EX + 1, 0:4 * EX + 1])\
                .then_inc(s_bct, 1)
            pe.wait_ge(s_wx, 2 * K2)

            def turn(t, q):
                pe.wait_ge(s_xn0, t + 1)
                for k in range(K2):
                    last = nc.tensor.transpose(PS[:, q, k * NP:(k + 1) * NP], xn[:, q, 128 * k:128 * k + 128],
                                               ident[0:NP, 0:NP])
                last.then_inc(s_xt0, 1)

            def product(t, q):
                pe.wait_ge(s_xe0, t + 1)
                for k in range(K2):
                    last = mm(PS[0:NP, 2 + q, 0:ROW + H], xT[:, q, k, :], wx[:, k, :], start=(k == 0),
                              stop=(k == K2 - 1))
                last.then_inc(s_h0, 1)

            turn(0, 0)
            turn(1, 1)
            product(0, 0)
            pe.wait_ge(s_xe0, 1)
            turn(2, 0)
            product(1, 1)
            with pe.Fori(1, (NW - 1) // 2) as i:
                pe.wait_ge(s_xe0, i * 2)
                turn(i * 2 + 1, 1)
                pe.wait_ge(s_hs, i * 2 - 1)
                product(i * 2, 0)
                pe.wait_ge(s_xe0, i * 2 + 1)
                turn(i * 2 + 2, 0)
                pe.wait_ge(s_hs, i * 2)
                product(i * 2 + 1, 1)
            pe.wait_ge(s_hs, NW - 2)
            product(NW - 1, 0)

            pe.wait_ge(s_ends, 1)
            for k in range(2):
                last = nc.tensor.transpose(PS[0:NW, 4, 128 * k:128 * k + 128], ends[:, k, :], ident[:, :])
            last.then_inc(s_endt, 1)
            pe.wait_ge(s_wplan, 1)
            for k in range(2):
                last = nc.tensor.transpose(PS[0:1, 4, 256 + NW * k:256 + NW * k + NW], wplan[:, k:k + 1],
                                           ident[0:NW, 0:NW])
            last.then_inc(s_plant, 1)

            most = most_passes(pe)
            x_no = counter(pe, "x_pe")
            pe.wait_ge(s_hs, NW)
            pe.wait_ge(s_bc, 1)
            pe.wait_ge(s_xe0, NW)

            def transposed(q, n, first, S):
                pe.wait_ge(S.onehot, n + 1)
                for g, cols in enumerate(T_GROUPS):
                    if g >= 2:
                        pe.wait_ge(S.ot, n * NG + (g - 1))
                    for k, j in enumerate(cols):
                        last = nc.tensor.transpose(PS[0:NP, g % 2, 128 * k:128 * k + 128], O[:, q, j, :],
                                                   ident[:, :])
                    last.then_inc(S.turned, 1)

            def candidates(t, q, n, S):
                pe.wait_ge(S.cand, n + 1)
                pe.wait_ge(S.ot, n * NG + (NG - 1))
                for j in range(NT):
                    mm(p_mid, O[:, q, j, :], t["mid"][:, j, :], start=(j == 0), stop=(j == NT - 1))
                dv = t["diag"][:, :, :, :].rearrange("p h k e -> p (h k e)")
                for b in range(2):
                    last = mm(p_cand[0:NP, 512 * b:512 * b + 512], ones[:, :], dv[:, 512 * b:512 * b + 512],
                              start=True, stop=True)
                last.then_inc(S.cands, 1)

            def spread(n, S):
                pe.wait_ge(S.nval, n + 1)
                pe.wait_ge(S.ot, (n + 1) * NG)
                for j in range(NT):
                    last = mm(p_spread[:, j, :, :].rearrange("p k h -> p (k h)"), OT[:, j, :],
                              nval[:, :, :].rearrange("p k h -> p (k h)"), start=True, stop=True)
                last.then_inc(S.spread, 1)

            def aggregate(q, n, S):
                pe.wait_ge(S.msg, n + 1)
                pe.wait_ge(S.den, n + 1)
                for j in range(NT):
                    last = mm(p_sum, O[:, q, j, :], MSG[:, j, :], start=(j == 0), stop=(j == NT - 1))
                last.then_inc(S.agg, 1)

            def pieces(u, a, b, first=False):
                for m in range(a, b):
                    kind, e = FFN[m]
                    if m >= 3:
                        dve, k = taken(m - 3)
                        pe.wait_ge(s_fd if dve else s_fa, u * (N_FD if dve else N_FA) + k)
                    elif m == 0 and not first:
                        pe.wait_ge(s_fd, u * N_FD)
                        pe.wait_ge(s_fa, u * N_FA)
                    ps = bank(m)

                    def ready(kind2, e2=0):
                        pe.wait_ge(s_fa, u * N_FA + taken(piece(kind2, e2))[1])

                    if kind == "turn":
                        pe.wait_ge(s_x1, u + 1)
                        for k in range(K2):
                            last = nc.tensor.transpose(ps[:, k * NP:(k + 1) * NP],
                                                       xn[:, 0, 128 * k:128 * k + 128], ident[0:NP, 0:NP])
                    elif kind == "hidden":
                        ready("turn")
                        for k in range(K2):
                            last = mm(ps[:, 0:NP], r1[:, k, :], xT[:, 0, k, :], start=(k == 0), stop=(k == 1))
                    elif kind == "logits":
                        ready("hidden")
                        last = mm(ps[0:NP, 0:EX], rhid[:, :], r2[:, :], start=True, stop=True)
                    elif kind in ("l1", "l2"):
                        ready(*(("turn",) if kind == "l1" else ("l1", e)))
                        wt, act_in = (w1, xT[:, 0, :, :]) if kind == "l1" else (w2, h1[:, e % 2, :, :])
                        for f in range(K2):
                            for k in range(K2):
                                last = mm(ps[:, f * NP:(f + 1) * NP], wt[:, e, k, 128 * f:128 * f + 128],
                                          act_in[:, k, :], start=(k == 0), stop=(k == 1))
                    elif kind == "turn_w":
                        pe.wait_ge(s_wts, u + 1)
                        last = nc.tensor.transpose(ps[0:8, 0:NP], wa[:, :], ident[0:NP, 0:NP])
                    elif kind == "bias3":
                        ready("turn_w")
                        last = mm(ps[0:NP, 0:D], wT[0:EX, :], b3[:, :], start=True, stop=True)
                    else:
                        ready("l2", e)
                        for k in range(K2):
                            last = mm(ps[0:NP, 0:D], h2[:, e, k, :], w3[:, e, k, :], start=(k == 0),
                                      stop=(k == 1))
                    last.then_inc(s_piece, 1)

            pe.wait_ge(s_we, 64)

            def window(v, prev, nxt, nxt2):
                w, q = v.w, v.q
                first = isinstance(w, int) and w == 1
                transposed(q, w, False, MAIN_S)
                candidates(MAIN_T, q, w, MAIN_S)
                if prev:
                    pieces(w - 1, 0, SPREAD_AT, first)
                spread(w, MAIN_S)
                if prev:
                    pieces(w - 1, SPREAD_AT, NF)
                aggregate(q, w, MAIN_S)

                def extra(n, c):
                    transposed(q, n, False, EXTRA_S)
                    candidates(EXTRA_T, q, n, EXTRA_S)
                    spread(n, EXTRA_S)
                    aggregate(q, n, EXTRA_S)

                extras(pe, most, x_no, w, extra)

            window(Win(0, 0, 0), False, True, True)
            window(Win(1, 1, 0), True, True, True)
            window(Win(2, 0, 1), True, True, True)
            with pe.Fori(1, (NW - 3) // 2) as i:
                window(Win(i * 2 + 1, 1, i), True, True, True)
                window(Win(i * 2 + 2, 0, i + 1), True, True, True)
            window(Win(NW - 2, 1, (NW - 2) // 2), True, True, False)
            window(Win(NW - 1, 0, (NW - 1) // 2), True, False, False)
            pieces(NW - 1, 0, NF)


_INS = ["x", "src", "dst", "L0_gnn_W", "L0_gnn_att_src", "L0_gnn_att_dst", "L0_gnn_bias", "L0_ffn_router_w1",
        "L0_ffn_router_b1", "L0_ffn_router_w2", "L0_ffn_router_b2", "L0_ffn_expert_w1", "L0_ffn_expert_b1",
        "L0_ffn_expert_w2", "L0_ffn_expert_b2", "L0_ffn_expert_w3", "L0_ffn_expert_b3"]


def kernel(**inputs):
    import numpy as _np
    import concourse.bacc as _bacc
    from concourse import mybir as _mybir
    from concourse.bass_utils import run_bass_kernel_spmd as _run

    nc = _bacc.Bacc("TRN2", target_bir_lowering=False, num_devices=1)
    arrays, args = {}, []
    for name in _INS:
        a = _np.ascontiguousarray(inputs[name])
        arrays[f"in_{name}_dram"] = a
        args.append(nc.dram_tensor(f"in_{name}_dram", a.shape, _mybir.dt.from_np(a.dtype), kind="ExternalInput").ap())
    args.append(nc.dram_tensor("out_0_dram", (N, D), _mybir.dt.float32, kind="ExternalOutput").ap())
    gat_ffn(nc, *args)
    r = _run(nc, [arrays], core_ids=[0])
    return r.results[0]["out_0_dram"]
```

```python
import concourse.bass as bass
from concourse import mybir
from collections import namedtuple
from contextlib import ExitStack


N, D, H, C = 3125, 256, 4, 64
NW, NP = 25, 125
E_IN = 53125
NT = 18
EC = 128 * NT
BLK = 8
NCOL = 416
NB_P = NCOL // BLK
NB = 128 * NB_P
E_PAD = 128 * NCOL + EC
PAD_DST = 4095
HC = C + 1
ROW = H * HC
K2 = D // 128
EX, RH = 6, 128
BIG = 1.0e30
EPS = 1e-5
SLOPE = 0.2
X_STEP = 5
STEPS = [(a, a + X_STEP) for a in range(0, NW, X_STEP)]
HALVES = ((0, 112), (112, NP))
T_GROUPS = [range(g, min(g + 6, NT)) for g in range(0, NT, 6)]
PARTS = 3
NG = len(T_GROUPS)
SQ = E_IN // NP
SORT_KEYS = 3125
SORT_CHUNKS = E_IN // SORT_KEYS
KEY_STEP = 4096

FFN = [("turn", 0), ("hidden", 0), ("l1", 0), ("logits", 0), ("l1", 1), ("l2", 0), ("l1", 2), ("l2", 1),
       ("l1", 3), ("l2", 2), ("l1", 4), ("l2", 3), ("l1", 5), ("l2", 4), ("turn_w", 0), ("l2", 5),
       ("bias3", 0), ("l3", 0), ("l3", 1), ("l3", 2), ("l3", 3), ("l3", 4), ("l3", 5)]
NF = len(FFN)
N_FA = NF - 1
BEFORE_SPREAD, BEFORE_SUM, BEFORE_RUNS, BEFORE_MAXIMA = 2, 10, 17, NF - 2
PEX_AFTER, E2_AFTER = ("l1", 1), ("l2", 2)

Win = namedtuple("Win", "w q half")


def piece(kind, e=0):
    return FFN.index((kind, e))


def taken(m):
    return m + 1 - (m >= piece("logits"))


def gat_ffn(nc, x, src, dst, w_gnn, att_src, att_dst, gnn_bias, rw1, rb1, rw2, rb2,
            ew1, eb1, ew2, eb2, ew3, eb3, out):
    f32, bf16, i32, u32 = mybir.dt.float32, mybir.dt.bfloat16, mybir.dt.int32, mybir.dt.uint32
    ALU, ACT, AX = mybir.AluOpType, mybir.ActivationFunctionType, mybir.AxisListType

    ctx = ExitStack()
    with ctx:
        def sb(name, shape, dt=f32):
            return ctx.enter_context(nc.sbuf_tensor(name, shape, dt))

        def sem(name):
            return ctx.enter_context(nc.semaphore(name))

        table = nc.dram_tensor("table", (N, ROW), f32, kind="Internal").ap()
        edges = nc.dram_tensor("edges", (E_PAD, 2), i32, kind="Internal").ap()

        ident = sb("ident", [128, 128])
        ident_b = sb("ident_b", [128, 128], bf16)
        ones = sb("ones", [128, NP])
        scrap = sb("scrap", [1, 1])
        tick = sb("tick", [1, 1])
        iota_n = sb("iota_n", [128, NP])
        wbase = sb("wbase", [128, NW + 1])
        pass_step = sb("pass_step", [1, NW])
        iota_e = sb("iota_e", [NP, 8])
        wx = sb("wx", [128, K2, ROW + H])
        att = sb("att", [128, 2, H, C])
        att_tmp = sb("att_tmp", [128, H, C])
        gbias = sb("gbias", [NP, D])
        rb2_b = sb("rb2_b", [NP, EX])
        brows = sb("brows", [4 * EX + 1, 128])
        bcols = sb("bcols", [128, 4 * EX + 1])
        b3 = sb("b3", [EX, D])
        r1 = sb("r1", [128, K2, RH])
        r2 = sb("r2", [RH, EX])
        w1 = sb("w1", [128, EX, K2, D])
        w2 = sb("w2", [128, EX, K2, D])
        w3 = sb("w3", [128, EX, K2, D])
        work = sb("work", [128, NT * (128 + ROW)])
        X = work[0:NP, 0:NW * D].rearrange("p (t d) -> p t d", d=D)
        xw = sb("xw", [NP, 2, D])
        HS = sb("HS", [NP, NW, ROW + H])
        EI = sb("EI", [128, 2, NT, 2], i32)
        XEI = sb("XEI", [128, NT, 2], i32)
        G = sb("G", [128, 2, NT, ROW])
        O = sb("O", [128, 2, NT, NP])
        OB = sb("OB", [128, NT, NP], bf16)
        OT = work[0:NP, 0:NT * 64].bitcast(bf16).rearrange("p (j e) -> p j e", e=128)
        MSG = work[:, NT * 128:NT * (128 + ROW)].rearrange("p (j r) -> p j r", r=ROW)

        def pass_tiles(s):
            t = {}
            for name, shape, dt in (("dstf", [128, NT], f32), ("same", [128, NT], f32), ("first", [128, NT], f32),
                                    ("inside", [128, NT], f32), ("pen", [128, H, NT], f32),
                                    ("a", [128, H, NT], f32), ("run", [128, H, NT], f32),
                                    ("fa", [128, H, NT], f32), ("cand", [128, 2, 2, H], f32),
                                    ("mid", [128, NT + 2, H + 1], f32),
                                    ("mid_b", [128, NT + 2, PARTS, H + 1], bf16)):
                t[name] = sb(f"{name}_{s}", shape, dt)
            return t

        MAIN_T, EXTRA_T = pass_tiles("m"), pass_tiles("x")
        row_same = sb("row_same", [H, 256])
        row_pen = sb("row_pen", [H, 256])
        row_run = sb("row_run", [H, 256])
        row_end = sb("row_end", [H, 256])
        cmid = sb("cmid", [NP, H + 1])
        cnone = sb("cnone", [NP, 1])
        cmax = sb("cmax", [NP, H])
        nmax = sb("nmax", [NP, H])
        nval = sb("nval", [NP, 2, H])
        nv = sb("nv", [NP, 2, H])
        nval_b = sb("nval_b", [NP, PARTS, 2, H], bf16)
        spd = sb("spd", [128, NT, 2, H])
        lold = sb("lold", [NP, H])
        own = sb("own", [NP, H])
        fac = sb("fac", [NP, H])
        al = sb("al", [128, NT, H])
        lr = sb("lr", [128, NT, H])
        ev = sb("ev", [128, NT, H])
        st = sb("st", [NP, ROW])
        rden = sb("rden", [NP, H])
        gat = sb("gat", [NP, D])
        terms = sb("terms", [NP, EX + 3, D])
        xn = sb("xn", [NP, 2, D])
        stats = sb("stats", [NP, NW, 6])
        mean = sb("mean", [NP, NW])
        rs = sb("rs", [NP, NW])
        rv = sb("rv", [NP, NW])
        rt = sb("rt", [NP, NW])
        mv = sb("mv", [NP, 2])
        xT = sb("xT", [128, 2, K2, NP])
        rhid = sb("rhid", [RH, NP])
        h1 = sb("h1", [128, 2, K2, NP])
        h2 = sb("h2", [128, EX, K2, NP])
        lg = sb("lg", [NP, EX])
        lmx = sb("lmx", [NP, 1])
        pex = sb("pex", [NP, EX])
        psm = sb("psm", [NP, 1])
        prob = sb("prob", [NP, 8])
        top = sb("top", [NP, 8])
        topi = sb("topi", [NP, 8], u32)
        topf = sb("topf", [NP, 2])
        gap = sb("gap", [NP, 1])
        e2 = sb("e2", [NP, 1])
        pw = sb("pw", [NP, 2])
        wa = sb("wa", [NP, 8])
        wb = sb("wb", [NP, 8])
        wT = sb("wT", [8, NP])
        yo = sb("yo", [NP, 2, D])
        pairs_in = G[0:NP, 0, 0:4, :].rearrange("p a b -> p (a b)")[:, 0:2 * SQ].bitcast(i32).rearrange(
            "p (s k) -> p s k", k=2)
        src_in = G[0:NP, 1, 0:4, :].rearrange("p a b -> p (a b)")[:, 0:SQ].bitcast(i32)
        dst_in = G[0:NP, 1, 0:4, :].rearrange("p a b -> p (a b)")[:, SQ:2 * SQ].bitcast(i32)
        n_pad = E_PAD - E_IN
        pads = sb("pads", [3, n_pad // 3, 2], i32)
        pairs = G[:, 0, 4:8, :].rearrange("p a b -> p (a b)")[:, 0:2 * NCOL].bitcast(i32).rearrange(
            "p (s k) -> p s k", k=2)
        o_flat = O[:, :, :, :].rearrange("p q j n -> p (q j n)")
        below_w = o_flat[:, 0:2 * NW * NB_P].rearrange("p (k w b) -> p k w b", k=2, b=NB_P)
        pass_of = o_flat[0:1, 0:NW * NW].rearrange("p (w c) -> p w c", c=NW)
        next_pair = sb("next_pair", [128, 2], i32)
        descents = o_flat[:, 0:NCOL]
        descended = sb("descended", [128, 1])
        unsorted = sb("unsorted", [1, 1], i32)
        g_flat = G[0:NP, :, :, :].rearrange("p q j r -> p (q j r)")
        hs_flat = HS[:, :, :].rearrange("p w r -> p (w r)")
        keys_in = o_flat[0:NP, 0:SORT_KEYS].bitcast(i32)
        keys, key_no = hs_flat[:, 0:SORT_KEYS], hs_flat[:, SORT_KEYS:2 * SORT_KEYS]
        below = g_flat[:, NT * ROW:NT * ROW + SORT_KEYS]
        edge_no, rank, threshold, n_below, rank_i = (
            g_flat[:, 8 * ROW + i * SQ:8 * ROW + (i + 1) * SQ] for i in range(5))
        rank_i = rank_i.bitcast(i32)
        move_to = sb("move_to", [NP, 1], i32)
        move = sb("move", [NP, 2], i32)
        bounds = sb("bounds", [128, 2, NW])
        span = sb("span", [1, 2 * NW])
        n_pass = sb("n_pass", [1, NW])
        most_f = sb("most_f", [1, 1])
        plan = sb("plan", [1, 2 * NW + 1], i32)

        PS = ctx.enter_context(nc.psum_tensor("PS", [128, 8, 512], f32))
        p_turned = [PS[0:NP, g, :].bitcast(bf16) for g in range(2)]
        p_row = PS[0:H, 2, :].rearrange("p (v i) -> p v i", v=2)
        p_back = PS[:, 2, 0:2 * (H + 1)].rearrange("p (k c) -> p k c", k=2)
        p_mid = PS[0:NP, 2, 16:16 + PARTS * (H + 1)]
        p_sum = PS[0:NP, 3, 0:ROW]
        p_spread = PS[:, 4, 0:NT * PARTS * 2 * H].rearrange("p (j s c) -> p j s c", s=PARTS, c=2 * H)

        def bank(m):
            return PS[:, 5 + m % 3, :]

        s_const = sem("s_const")
        s_x = [sem(f"s_xin{i}") for i in range(len(STEPS))]
        s_ein = sem("s_ein")
        s_pairs = sem("s_pairs")
        s_edged = sem("s_edged")
        s_back = sem("s_back")
        s_descents = sem("s_descents")
        s_descsum = sem("s_descsum")
        s_order = sem("s_order")
        s_numbers = sem("s_numbers")
        s_keys = sem("s_keys")
        s_keys_used = sem("s_keys_used")
        s_ranks = sem("s_ranks")
        s_moved = sem("s_moved")
        s_sorted = sem("s_sorted")
        s_resorted = sem("s_resorted")
        s_wg = sem("s_wg")
        s_wb = sem("s_wb")
        s_we = sem("s_we")
        s_chain = sem("s_chain")
        s_tick = sem("s_tick")
        s_stats = sem("s_stats")
        s_wx = sem("s_wx")
        s_bounds = sem("s_bounds")
        s_span = sem("s_span")
        s_plan = sem("s_plan")
        s_bct = sem("s_bct")
        s_bc = sem("s_bc")
        s_xn0 = sem("s_xn0")
        s_xt0 = sem("s_xt0")
        s_xe0 = sem("s_xe0")
        s_h0 = sem("s_h0")
        s_hs = sem("s_hs")
        s_table = sem("s_table")
        s_load = [sem("s_load0"), sem("s_load1")]
        s_xw = [sem("s_xw0"), sem("s_xw1")]
        s_gath = [sem("s_gath0"), sem("s_gath1")]
        s_out = [sem("s_out0"), sem("s_out1")]
        s_x1 = sem("s_x1")
        s_piece = sem("s_piece")
        s_fa = sem("s_fa")
        s_fd = sem("s_fd")
        s_done = sem("s_done")
        s_lgm = sem("s_lgm")
        s_pex = sem("s_pex")
        s_gap = sem("s_gap")
        s_e2 = sem("s_e2")
        s_wts = sem("s_wts")

        Sems = namedtuple("Sems", "onehot ob turned ot cand row ends back mid mids nval spread old fac zed ev den "
                                  "msg agg merged")

        def pass_sems(s):
            return Sems(*[sem(f"s_{n}_{s}") for n in Sems._fields])

        MAIN_S, EXTRA_S = pass_sems("m"), pass_sems("x")
        s_xload = sem("s_xload")
        s_xgath = sem("s_xgath")

        block = ctx.enter_context(nc.Block())

        def row(t, w):
            return t[:, bass.ds(w, 1), :].rearrange("p a d -> p (a d)")

        def most_passes(eng):
            eng.wait_ge(s_plan, 1)
            return eng.value_load(plan[0:1, 2 * NW:2 * NW + 1], min_val=1, max_val=NW)

        def is_unsorted(eng):
            eng.wait_ge(s_order, 1)
            return eng.value_load(unsorted[0:1, 0:1], min_val=0, max_val=128)

        def extras(eng, most, x, w, body):
            with eng.If(most > 1):
                n = eng.value_load(plan[0:1, bass.ds(NW + w, 1)], min_val=1, max_val=NW)
                with eng.If(n > 1):
                    with eng.Fori(1, n) as c:
                        body(eng.snap(x), c)
                        eng.reg_add(x, x, 1)

        def windows(body):
            def run(eng):
                body(Win(0, 0, 0), False, True, True)
                with eng.Fori(0, (NW - 3) // 2) as i:
                    body(Win(i * 2 + 1, 1, i), True, True, True)
                    body(Win(i * 2 + 2, 0, i + 1), True, True, True)
                body(Win(NW - 2, 1, (NW - 2) // 2), True, True, False)
                body(Win(NW - 1, 0, (NW - 1) // 2), True, False, False)
            return run

        def val(eng, v):
            return v if isinstance(v, int) else eng.to_reg(v)

        def counter(eng, name):
            x = eng.alloc_register(name)
            eng.reg_mov(x, 0)
            return x

        @block.sync
        def _(sp):
            sp.dma_start(src_in, src.rearrange("(p s) -> p s", p=NP)).then_inc(s_ein, 16)
            sp.dma_start(dst_in, dst.rearrange("(p s) -> p s", p=NP)).then_inc(s_ein, 16)
            xv = x.rearrange("(t p) d -> p t d", p=NP)
            def load_steps(steps):
                for c, d in steps:
                    for a, b in HALVES:
                        sp.dma_start(X[a:b, c:d, :], xv[a:b, c:d, :]).then_inc(s_x[c // X_STEP], 16)

            load_steps(STEPS[0:1])
            sp.wait_ge(s_pairs, 2)
            sp.wait_ge(s_const, 2)
            sp.dma_start(edges[0:E_IN, :].rearrange("(p s) k -> p (s k)", p=NP),
                         pairs_in.rearrange("p s k -> p (s k)")).then_inc(s_edged, 16)
            sp.dma_start(edges[E_IN:E_PAD, :].rearrange("(p s) k -> p (s k)", p=3),
                         pads[:, :, :].rearrange("p s k -> p (s k)")).then_inc(s_edged, 16)
            load_steps(STEPS[1:2])
            sp.wait_ge(s_edged, 32)
            sp.dma_start(pairs.rearrange("p s k -> p (s k)"),
                         edges[0:128 * NCOL, :].rearrange("(p s) k -> p (s k)", p=128)).then_inc(s_back, 16)
            sp.dma_start(next_pair[:, :], edges[NCOL:129 * NCOL, :].rearrange("(p s) k -> p s k", p=128)[:, 0, :])\
                .then_inc(s_back, 16)
            load_steps(STEPS[2:])
            with sp.If(is_unsorted(sp) > 0):
                with sp.Fori(0, SORT_CHUNKS) as c:
                    used, at = val(sp, c + 1), c * SORT_KEYS
                    val(sp, at * 4)
                    sp.wait_ge(s_keys_used, used)
                    sp.dma_start(keys_in, dst[bass.ds(at, SORT_KEYS)].partition_broadcast(NP)).then_inc(s_keys, 16)
                sp.wait_ge(s_sorted, 1)
                sp.dma_start(pairs.rearrange("p s k -> p (s k)"),
                             edges[0:128 * NCOL, :].rearrange("(p s) k -> p (s k)", p=128)).then_inc(s_resorted, 16)
            tv = table.rearrange("(t p) r -> p t r", p=NP)
            for c, d in STEPS:
                sp.wait_ge(s_hs, d)
                for a, b in HALVES:
                    sp.dma_start(tv[a:b, c:d, :], HS[a:b, c:d, 0:ROW]).then_inc(s_table, 16)

            edge_list = edges.rearrange("e k -> (e k)")
            x_list, out_list = x.rearrange("n d -> (n d)"), out.rearrange("n d -> (n d)")
            most = most_passes(sp)
            x_no = counter(sp, "x_sp")

            def first_edge(w):
                return offset(sp.value_load(plan[0:1, bass.ds(w, 1)], min_val=0, max_val=2 * BLK * NB))

            def offset(v):
                val(sp, v * 4)
                return v

            def load(e0, q):
                sp.dma_start(EI[:, q, :, :].rearrange("p j k -> p (j k)"),
                             edge_list[bass.ds(e0, 2 * EC)].rearrange("(p j) -> p j", p=128))\
                    .then_inc(s_load[q], 16)

            def window(v, prev, nxt, nxt2):
                if nxt2:
                    gathered, seen = val(sp, 16 * NT * (v.half + 1)), val(sp, v.w + 1)
                    e0 = first_edge(v.w + 2)
                    sp.wait_ge(s_gath[v.q], gathered)
                    sp.wait_ge(MAIN_S.onehot, seen)
                    load(e0, v.q)

                def extra(n, c):
                    e0 = first_edge(v.w)
                    start = nc.s_assert_within(e0 + c * (2 * EC), 0, 2 * BLK * NB, skip_runtime_bounds_check_because=
                                               "a pass starts before the window's last edge")
                    start, main, before = offset(start), val(sp, v.w + 1), val(sp, n + 1)
                    sp.wait_ge(MAIN_S.merged, main)
                    sp.wait_ge(EXTRA_S.merged, before)
                    sp.dma_start(XEI[:, :, :].rearrange("p j k -> p (j k)"),
                                 edge_list[bass.ds(start, 2 * EC)].rearrange("(p j) -> p j", p=128))\
                        .then_inc(s_xload, 16)

                extras(sp, most, x_no, v.w, extra)
                if nxt:
                    if prev:
                        used = val(sp, v.w)
                    at = offset((v.w + 1) * (NP * D))
                    if prev:
                        sp.wait_ge(s_x1, used)
                    load_x(at, 1 - v.q)
                if prev:
                    store(v.w - 1, 1 - v.q)

            def store(w, q):
                done, at = val(sp, w + 1), offset(w * (NP * D))
                sp.wait_ge(s_done, done)
                sp.dma_start(out_list[bass.ds(at, NP * D)].rearrange("(p d) -> p d", p=NP), yo[:, q, :]).then_inc(s_out[q], 16)

            def load_x(at, q):
                sp.dma_start(xw[:, q, :], x_list[bass.ds(at, NP * D)].rearrange("(p d) -> p d", p=NP)).then_inc(s_xw[q], 16)

            load(first_edge(0), 0)
            load(first_edge(1), 1)
            load_x(0, 0)
            windows(window)(sp)
            store(NW - 1, (NW - 1) % 2)
            sp.wait_ge(s_out[0], 16 * ((NW + 1) // 2))
            sp.wait_ge(s_out[1], 16 * (NW // 2))
            sp.wait_ge(s_table, 32 * len(STEPS))

        @block.gpsimd
        def _(pool):
            pool.memset(pads[:, :, 0:1], 0).then_inc(s_const, 1)
            pool.memset(pads[:, :, 1:2], PAD_DST).then_inc(s_const, 1)
            pool.memset(ident[:, :], 0.0).then_inc(s_const, 1)
            pool.wait_ge(s_const, 3)
            pool.affine_select(out=ident[:, :], in_=ident[:, :], compare_op=ALU.not_equal, fill=1.0, base=0,
                               pattern=[[-1, 128]], channel_multiplier=1).then_inc(s_const, 1)
            pool.wait_ge(s_const, 4)
            pool.memset(tick[:, :], 0.0).then_inc(s_const, 1)
            pool.memset(ones[:, :], 1.0).then_inc(s_const, 1)
            pool.tensor_copy(ident_b[:, :], ident[:, :]).then_inc(s_const, 1)

            def hold():
                pool.tensor_tensor(tick[:, :], tick[:, :], tick[:, :], ALU.mult).then_inc(s_tick, 1)
                pool.wait_ge(s_tick, 1)
                pool.sem_clear(s_tick)

            def count(t, step, n, base=0, mult=0):
                pool.iota(t, pattern=[[step, n]], base=base, channel_multiplier=mult,
                          allow_small_or_imprecise_dtypes=True).then_inc(s_const, 1)

            count(iota_n[:, :], 1, NP)
            count(wbase[:, :], NP, NW + 1)
            count(pass_step[:, :], EC // BLK, NW)
            count(iota_e[:, :], 1, 8)

            pool.wait_ge(s_const, 11)
            with pool.If(is_unsorted(pool) > 0):
                pool.iota(key_no, pattern=[[1, SORT_KEYS]], base=0, channel_multiplier=0,
                          allow_small_or_imprecise_dtypes=True).then_inc(s_numbers, 1)
                pool.iota(edge_no, pattern=[[1, SQ]], base=0, channel_multiplier=SQ,
                          allow_small_or_imprecise_dtypes=True).then_inc(s_numbers, 1)
                pool.wait_ge(s_ranks, 1)
                hold()
                with pool.Fori(0, SQ) as s:
                    pool.tensor_copy(move_to[:, :], rank_i[:, bass.ds(s, 1)]).then_inc(s_tick, 1)
                    pool.tensor_copy(move[:, :], pairs_in[:, bass.ds(s, 1), :].rearrange("p a k -> p (a k)"))\
                        .then_inc(s_tick, 1)
                    pool.wait_ge(s_tick, 2)
                    pool.sem_clear(s_tick)
                    pool.indirect_dma_start(edges, bass.IndirectOffsetOnAxis(ap=move_to[:, 0:1], axis=0),
                                            move[:, :], None).then_inc(s_moved, 16)
                    pool.wait_ge(s_moved, s * 16 + 16)
                    hold()
                pool.tensor_tensor(tick[:, :], tick[:, :], tick[:, :], ALU.mult).then_inc(s_sorted, 1)
            most = most_passes(pool)
            x_no = counter(pool, "x_pool")
            pool.wait_ge(s_table, 32 * len(STEPS))

            def gather(idx, q, done):
                for j in range(NT):
                    pool.indirect_dma_start(
                        G[:, q, j, :], None, table,
                        bass.IndirectOffsetOnAxis(ap=idx[:, j, 0:1], axis=0)).then_inc(done, 16)

            def window(v, prev, nxt, nxt2):
                if nxt:
                    loaded, used = val(pool, 16 * (v.half + v.q + 1)), val(pool, v.w)
                    pool.wait_ge(s_load[1 - v.q], loaded)
                    hold()
                    if prev:
                        pool.wait_ge(MAIN_S.msg, used)
                        hold()
                    gather(EI[:, 1 - v.q, :, :], 1 - v.q, s_gath[1 - v.q])

                def extra(n, c):
                    pool.wait_ge(s_xload, (n + 1) * 16)
                    hold()
                    gather(XEI, v.q, s_xgath)
                    pool.wait_ge(EXTRA_S.msg, n + 1)
                    hold()

                extras(pool, most, x_no, v.w, extra)

            pool.wait_ge(s_load[0], 16)
            gather(EI[:, 0, :, :], 0, s_gath[0])
            windows(window)(pool)

        @block.vector
        def _(dve):
            v_ = nc.vector
            links = [0]

            def link(ins):
                links[0] += 1
                ins.then_inc(s_chain, 1)
                dve.wait_ge(s_chain, links[0])

            def tell(ins, done, n):
                ins.then_inc(done, 1)
                dve.wait_ge(done, n)

            def settle():
                link(v_.memset(scrap[:, :], 0.0))
                relink()

            def relink():
                dve.sem_clear(s_chain)
                links[0] = 0

            def rsqrt(r, var, v, t):
                link(v_.tensor_scalar(v, var, EPS, None, ALU.add))
                link(v_.tensor_scalar(r.bitcast(i32), v.bitcast(i32), -0.5, 1597463007.0, ALU.mult, ALU.add))
                link(v_.tensor_scalar(v, v, -0.5, None, ALU.mult))
                for _ in range(3):
                    link(v_.tensor_tensor(t, r, r, ALU.mult))
                    link(v_.tensor_tensor(t, t, v, ALU.mult))
                    link(v_.scalar_tensor_tensor(r, t, 1.5, r, ALU.add, ALU.mult))

            def split(parts, t, left):
                link(v_.tensor_copy(parts[0], t))
                link(v_.tensor_tensor(left, t, parts[0], ALU.subtract))
                link(v_.tensor_copy(parts[1], left))
                return lambda: v_.tensor_tensor(parts[2], left, parts[1], ALU.subtract)

            dve.wait_ge(s_ein, 32)
            tell(v_.tensor_copy(pairs_in[:, :, 0], src_in), s_pairs, 1)
            tell(v_.tensor_copy(pairs_in[:, :, 1], dst_in), s_pairs, 2)
            for t in (MAIN_T, EXTRA_T):
                link(v_.memset(t["same"][:, 0:1], 0.0))
                link(v_.memset(t["first"][:, 0:1], 1.0))
                link(v_.memset(t["inside"][:, NT - 1:NT], 0.0))
            link(v_.memset(row_same[:, 0:1], 0.0))
            link(v_.memset(row_end[:, 255:256], 1.0))
            tell(v_.memset(prob[:, EX:8], -1.0), EXTRA_S.merged, 1)

            dve.wait_ge(s_wg, 64)
            for k in range(K2):
                wk = wx[:, k, 0:ROW].rearrange("p (h c) -> p h c", c=HC)
                for a in range(2):
                    link(v_.tensor_tensor(att_tmp[:, :, :], wk[:, :, 0:C], att[:, a, :, :], ALU.mult))
                    to = wk[:, :, C:HC].rearrange("p h c -> p (h c)") if a == 0 else wx[:, k, ROW:ROW + H]
                    tell(v_.tensor_reduce(to, att_tmp[:, :, :], AX.X, ALU.add), s_wx, 2 * k + a + 1)

            dve.wait_ge(s_back, 32)
            link(v_.tensor_tensor(descents[:, 1:NCOL], pairs[:, 1:NCOL, 1], pairs[:, 0:NCOL - 1, 1], ALU.is_lt))
            link(v_.tensor_tensor(descents[:, 0:1], next_pair[:, 1:2], pairs[:, NCOL - 1:NCOL, 1], ALU.is_lt))
            tell(v_.tensor_reduce(descended[:, :], descents, AX.X, ALU.max), s_descents, 1)
            dve.wait_ge(s_descsum, 1)
            tell(v_.tensor_copy(unsorted[:, :], bank(2)[0:1, 0:1]), s_order, 1)
            relink()
            with dve.If(is_unsorted(dve) > 0):
                tell(v_.memset(rank, 0.0), s_keys_used, 1)
                dve.wait_ge(s_numbers, 2)
                with dve.Fori(0, SORT_CHUNKS) as c:
                    dve.wait_ge(s_keys, c * 16 + 16)
                    tell(v_.scalar_tensor_tensor(keys, keys_in, float(KEY_STEP), key_no, ALU.mult, ALU.add),
                         s_keys_used, c + 2)
                    link(v_.tensor_scalar(threshold, edge_no, 0.0, float(KEY_STEP - 1), ALU.max, ALU.min))
                    link(v_.scalar_tensor_tensor(threshold, pairs_in[:, :, 1], float(KEY_STEP), threshold,
                                                 ALU.mult, ALU.add))
                    link(v_.tensor_scalar(edge_no, edge_no, float(SORT_KEYS), None, ALU.subtract))
                    relink()
                    with dve.Fori(0, SQ) as s:
                        link(v_.tensor_scalar(below, keys, threshold[:, bass.ds(s, 1)], None, ALU.is_lt))
                        link(v_.tensor_reduce(n_below[:, bass.ds(s, 1)], below, AX.X, ALU.add))
                        relink()
                    link(v_.tensor_tensor(rank, rank, n_below, ALU.add))
                    relink()
                tell(v_.tensor_copy(rank_i, rank), s_ranks, 1)
                dve.wait_ge(s_resorted, 16)
                settle()

            dve.wait_ge(s_const, 11)
            for k, at in enumerate((BLK - 1, 0)):
                blocks = pairs[:, at:NCOL:BLK, 1].unsqueeze(1).broadcast_to([128, NW, NB_P])
                limits = wbase[:, k:k + NW].unsqueeze(2).broadcast_to([128, NW, NB_P])
                link(v_.tensor_tensor(below_w[:, k, :, :], blocks, limits, ALU.is_lt))
            tell(v_.tensor_reduce(bounds[:, :, :].rearrange("p k w -> p (k w)"),
                                  below_w.rearrange("p k w b -> p (k w) b"), AX.X, ALU.add), s_bounds, 1)
            dve.wait_ge(s_span, 1)
            link(v_.tensor_copy(span[:, :], PS[0:1, 4, 0:2 * NW]))
            link(v_.tensor_tensor(n_pass[:, :], span[:, NW:2 * NW], span[:, 0:NW], ALU.subtract))
            link(v_.tensor_tensor(pass_of, pass_step[:, :].unsqueeze(1).broadcast_to([1, NW, NW]),
                                  n_pass[:, :].unsqueeze(2).broadcast_to([1, NW, NW]), ALU.is_lt))
            link(v_.tensor_reduce(n_pass[:, :], pass_of, AX.X, ALU.add))
            link(v_.tensor_scalar(n_pass[:, :], n_pass[:, :], 1.0, None, ALU.max))
            link(v_.tensor_reduce(most_f[:, :], n_pass[:, :], AX.X, ALU.max))
            link(v_.tensor_scalar(plan[0:1, 0:NW], span[:, 0:NW], float(2 * BLK), None, ALU.mult))
            link(v_.tensor_copy(plan[0:1, NW:2 * NW], n_pass[:, :]))
            relink()
            tell(v_.tensor_copy(plan[0:1, 2 * NW:2 * NW + 1], most_f[:, :]), s_plan, 1)

            for i, (c, d) in enumerate(STEPS):
                dve.wait_ge(s_x[i], 32)
                for t in range(c, d):
                    v_.bn_stats(row(stats, t), row(X, t)).then_inc(s_stats, 1)
            dve.wait_ge(s_stats, NW)
            link(v_.tensor_tensor(mean[:, :], stats[:, :, 1], stats[:, :, 4], ALU.add))
            link(v_.tensor_tensor(rt[:, :], stats[:, :, 1], stats[:, :, 4], ALU.subtract))
            link(v_.tensor_tensor(rt[:, :], rt[:, :], rt[:, :], ALU.mult))
            link(v_.tensor_tensor(rv[:, :], stats[:, :, 2], stats[:, :, 5], ALU.add))
            link(v_.scalar_tensor_tensor(rv[:, :], rt[:, :], float(D // 4), rv[:, :], ALU.mult, ALU.add))
            link(v_.tensor_scalar(rv[:, :], rv[:, :], 1.0 / D, None, ALU.mult))
            link(v_.tensor_scalar(mean[:, :], mean[:, :], 0.5, None, ALU.mult))
            rsqrt(rs[:, :], rv[:, :], rv[:, :], rt[:, :])
            relink()

            def normalise(t, q):
                tell(v_.tensor_scalar(xn[:, q, :], row(X, t), mean[:, bass.ds(t, 1)], rs[:, bass.ds(t, 1)],
                                 ALU.subtract, ALU.mult), s_xn0, t + 1)

            def keep_h(t, q):
                dve.wait_ge(s_h0, t + 1)
                tell(v_.tensor_copy(row(HS, t), PS[0:NP, 2 + q, 0:ROW + H]), s_hs, t + 1)

            normalise(0, 0)
            normalise(1, 1)
            with dve.Fori(0, (NW - 2) // 4) as i:
                for k in range(4):
                    dve.wait_ge(s_xt0, i * 4 + k + 1)
                    normalise(i * 4 + k + 2, k % 2)
                    keep_h(i * 4 + k, k % 2)
                settle()
            for t in range((NW - 2) // 4 * 4, NW):
                if t + 2 < NW:
                    dve.wait_ge(s_xt0, t + 1)
                    normalise(t + 2, t % 2)
                keep_h(t, t % 2)

            most = most_passes(dve)
            x_no = counter(dve, "x_dve")

            def edges_of(t, ei, o, w, n, S):
                link(v_.tensor_scalar(t["dstf"][:, :], ei[:, :, 1], wbase[:, bass.ds(w, 1)], None, ALU.subtract))
                tell(v_.tensor_tensor(o, iota_n[:, :].unsqueeze(1).broadcast_to([128, NT, NP]),
                                 t["dstf"][:, :].unsqueeze(2).broadcast_to([128, NT, NP]),
                                 ALU.is_equal), S.onehot, n + 1)
                link(v_.tensor_tensor(t["same"][:, 1:NT], t["dstf"][:, 1:NT], t["dstf"][:, 0:NT - 1],
                                      ALU.is_equal))
                link(v_.tensor_scalar(t["pen"][:, :, :], t["same"][:, :].unsqueeze(1).broadcast_to([128, H, NT]),
                                 -1.0, BIG, ALU.add, ALU.mult))
                link(v_.tensor_tensor_scan(t["first"][:, 1:NT], t["same"][:, 1:NT], t["same"][:, 1:NT], 1.0,
                                           ALU.mult, ALU.mult))
                link(v_.tensor_scalar(t["inside"][:, 0:NT - 1], t["first"][:, 0:NT - 1], -1.0, None, ALU.add))
                link(v_.scalar_tensor_tensor(t["inside"][:, 0:NT - 1], t["same"][:, 1:NT], -1.0,
                                             t["inside"][:, 0:NT - 1], ALU.add, ALU.mult))

            def candidates(t, g, n, S):
                gv = g.rearrange("p j (h c) -> p h j c", c=HC)[:, :, :, C]
                link(v_.tensor_copy(t["a"][:, :, :], gv))
                flat = "p h j -> p (h j)"
                link(v_.tensor_tensor_scan(t["run"][:, :, :].rearrange(flat), t["pen"][:, :, :].rearrange(flat),
                                           t["a"][:, :, :].rearrange(flat), -BIG, ALU.add, ALU.max))
                link(v_.tensor_scalar(t["fa"][:, :, :],
                                      t["first"][:, :].unsqueeze(1).broadcast_to([128, H, NT]),
                                      -1.0, BIG, ALU.add, ALU.mult))
                link(v_.tensor_tensor(t["fa"][:, :, :], t["fa"][:, :, :], t["a"][:, :, :], ALU.add))
                link(v_.tensor_copy(t["cand"][:, 1, 0, :], t["run"][:, :, NT - 1]))
                link(v_.tensor_copy(t["cand"][:, :, 1, :],
                                    t["dstf"][:, 0:NT:NT - 1].unsqueeze(2).broadcast_to([128, 2, H])))
                tell(v_.tensor_reduce(t["cand"][:, 0, 0, :], t["fa"][:, :, :], AX.X, ALU.max), S.cand, n + 1)
                link(v_.tensor_tensor(t["mid"][:, 0:NT, 0:H], t["run"][:, :, :].rearrange("p h j -> p j h"),
                                 t["inside"][:, :].unsqueeze(2).broadcast_to([128, NT, H]), ALU.mult))
                link(v_.tensor_copy(t["mid"][:, 0:NT, H], t["inside"][:, :]))

            def across(n, S):
                dve.wait_ge(S.row, n + 1)
                values, nodes = p_row[:, 0, :], p_row[:, 1, :]
                link(v_.tensor_copy(row_run[:, :], nodes))
                link(v_.tensor_tensor(row_same[:, 1:256], row_run[:, 1:256], row_run[:, 0:255], ALU.is_equal))
                link(v_.tensor_scalar(row_pen[:, :], row_same[:, :], -1.0, BIG, ALU.add, ALU.mult))
                link(v_.tensor_scalar(row_end[:, 0:255], row_same[:, 1:256], -1.0, 1.0, ALU.mult, ALU.add))
                link(v_.tensor_tensor_scan(row_run[:, :], row_pen[:, :], values, -BIG, ALU.add, ALU.max))
                tell(v_.tensor_tensor(row_run[:, :], row_run[:, :], row_end[:, :], ALU.mult), S.ends, n + 1)

            def runs(t, n, S):
                dve.wait_ge(S.back, n + 1)
                link(v_.tensor_copy(t["mid"][:, NT:NT + 2, :], p_back))
                parts = [t["mid_b"][:, :, s, :] for s in range(PARTS)]
                tell(split(parts, t["mid"][:, :, :], t["mid"][:, :, :])(), S.mid, n + 1)

            def maxima(w, n, first, S):
                hs = row(HS, w)
                a_dst = hs[:, ROW:ROW + H]
                old = hs[:, 0:ROW].rearrange("p (h c) -> p h c", c=HC)[:, :, C] if first else nmax[:, :]
                if not first:
                    link(v_.tensor_copy(lold[:, :], nval[:, 1, :]))
                link(v_.tensor_copy(nval[:, 0, :], a_dst))
                dve.wait_ge(S.mids, n + 1)
                link(v_.tensor_reduce(cmid[:, :], p_mid.rearrange("p (s c) -> p c s", s=PARTS), AX.X, ALU.add))
                link(v_.tensor_scalar(cnone[:, :], cmid[:, H:H + 1], -1.0, BIG, ALU.add, ALU.mult))
                link(v_.scalar_tensor_tensor(nmax[:, :], cmid[:, 0:H], cnone[:, :], old, ALU.add, ALU.max))
                link(v_.tensor_tensor(cmax[:, :], nmax[:, :], a_dst, ALU.add))
                link(v_.scalar_tensor_tensor(nval[:, 1, :], cmax[:, :], SLOPE, cmax[:, :], ALU.mult, ALU.max))
                lo = split([nval_b[:, s, :, :] for s in range(PARTS)], nval[:, :, :], nv[:, :, :])
                relink()
                lo().then_inc(S.nval, 1)

            def rescale(w, n, first, S):
                if first:
                    hs = row(HS, w)
                    a_src = hs[:, 0:ROW].rearrange("p (h c) -> p h c", c=HC)[:, :, C]
                    link(v_.tensor_tensor(own[:, :], a_src, hs[:, ROW:ROW + H], ALU.add))
                    link(v_.scalar_tensor_tensor(lold[:, :], own[:, :], SLOPE, own[:, :], ALU.mult, ALU.max))
                tell(v_.tensor_tensor(lold[:, :], lold[:, :], nval[:, 1, :], ALU.subtract), S.old, n + 1)

            def exponents(t, n, S):
                dve.wait_ge(S.spread, n + 1)
                link(v_.tensor_reduce(spd[:, :, :, :].rearrange("p j k h -> p j (k h)"),
                                      p_spread.rearrange("p j s c -> p j c s"), AX.X, ALU.add))
                link(v_.tensor_tensor(al[:, :, :], t["a"][:, :, :].rearrange("p h j -> p j h"),
                                      spd[:, :, 0, :], ALU.add))
                link(v_.scalar_tensor_tensor(lr[:, :, :], al[:, :, :], SLOPE, al[:, :, :], ALU.mult, ALU.max))
                link(v_.tensor_tensor(lr[:, :, :], lr[:, :, :], spd[:, :, 1, :], ALU.subtract))
                tell(v_.tensor_scalar(lr[:, :, :], lr[:, :, :], 0.0, None, ALU.min), S.zed, n + 1)

            def messages(g, n, S):
                dve.wait_ge(S.ev, n + 1)
                tell(v_.tensor_tensor(MSG[:, :, :].rearrange("p j (h c) -> p (j h) c", c=HC)[:, :, 0:C],
                                 g.rearrange("p j (h c) -> p (j h) c", c=HC)[:, :, 0:C],
                                 ev[:, :, :].rearrange("p j h -> p (j h)").unsqueeze(2)
                                 .broadcast_to([128, NT * H, C]), ALU.mult), S.msg, n + 1)

            def merge(w, n, first, S):
                dve.wait_ge(S.fac, n + 1)
                s3 = st[:, :].rearrange("p (h c) -> p h c", c=HC)
                old = row(HS, w)[:, 0:ROW].rearrange("p (h c) -> p h c", c=HC) if first else s3
                link(v_.tensor_tensor(s3, old, fac[:, :].unsqueeze(2).broadcast_to([NP, H, HC]), ALU.mult))
                if first:
                    link(v_.tensor_copy(s3[:, :, C], fac[:, :]))
                relink()
                dve.wait_ge(S.agg, n + 1)
                v_.tensor_tensor(st[:, :], st[:, :], p_sum, ALU.add).then_inc(S.merged, 1)
                if not first:
                    dve.wait_ge(S.merged, n + 2)
                    settle()

            def finish(w, q, half):
                dve.wait_ge(MAIN_S.merged, w + 1)
                s3 = st[:, :].rearrange("p (h c) -> p h c", c=HC)
                link(v_.tensor_scalar(rden[:, :], s3[:, :, C], 1e-16, None, ALU.add))
                link(v_.reciprocal(rden[:, :], rden[:, :]))
                link(v_.tensor_tensor(gat[:, :].rearrange("p (h c) -> p h c", c=C), s3[:, :, 0:C],
                                      rden[:, :].unsqueeze(2).broadcast_to([NP, H, C]), ALU.mult))
                link(v_.tensor_tensor(gat[:, :], gat[:, :], gbias[:, :], ALU.add))
                dve.wait_ge(s_xw[q], 16 * (half + 1))
                x1 = terms[:, q * (EX + 2), :]
                link(v_.scalar_tensor_tensor(x1, gat[:, :], 0.0, xw[:, q, :], ALU.max, ALU.add))
                link(v_.bn_stats(stats[:, 0, :], x1))
                link(v_.bn_aggr(mv[:, :], stats[:, 0, :]))
                rsqrt(rs[:, 0:1], mv[:, 1:2], rv[:, 0:1], rt[:, 0:1])
                relink()
                v_.tensor_scalar(xn[:, 0, :], x1, mv[:, 0:1], rs[:, 0:1],
                                 ALU.subtract, ALU.mult).then_inc(s_x1, 1)

            def route_logits(u):
                m = piece("logits")
                dve.wait_ge(s_piece, u * NF + m + 1)
                tell(v_.tensor_tensor(lg[:, :], bank(m)[0:NP, 0:EX], rb2_b[:, :], ALU.add), s_fd, u + 1)
                link(v_.tensor_reduce(lmx[:, :], lg[:, :], AX.X, ALU.max))
                tell(v_.tensor_scalar(lg[:, :], lg[:, :], lmx[:, :], None, ALU.subtract), s_lgm, u + 1)

            def route_best(u):
                dve.wait_ge(s_pex, u + 1)
                link(v_.tensor_reduce(psm[:, :], pex[:, :], AX.X, ALU.add))
                link(v_.reciprocal(psm[:, :], psm[:, :]))
                link(v_.tensor_scalar(prob[:, 0:EX], pex[:, :], psm[:, :], None, ALU.mult))
                link(v_.max(top[:, :], prob[:, :]))
                link(v_.max_index(topi[:, :], top[:, :], prob[:, :]))
                tell(v_.tensor_tensor(gap[:, :], top[:, 1:2], top[:, 0:1], ALU.subtract), s_gap, u + 1)
                link(v_.tensor_copy(topf[:, :], topi[:, 0:2]))

            def route_weights(u):
                dve.wait_ge(s_e2, u + 1)
                link(v_.tensor_scalar(pw[:, 0:1], e2[:, :], 1.0, None, ALU.add))
                link(v_.reciprocal(pw[:, 0:1], pw[:, 0:1]))
                link(v_.tensor_tensor(pw[:, 1:2], e2[:, :], pw[:, 0:1], ALU.mult))
                link(v_.tensor_scalar(wa[:, :], iota_e[:, :], topf[:, 0:1], pw[:, 0:1], ALU.is_equal, ALU.mult))
                link(v_.tensor_scalar(wb[:, :], iota_e[:, :], topf[:, 1:2], pw[:, 1:2], ALU.is_equal, ALU.mult))
                tell(v_.tensor_tensor(wa[:, :], wa[:, :], wb[:, :], ALU.add), s_wts, u + 1)

            def combine(u, q, half):
                dve.wait_ge(s_fa, (u + 1) * N_FA)
                if half is not None:
                    dve.wait_ge(s_out[q], 16 * half)
                v_.tensor_reduce(yo[:, q, :], terms[:, q:q + EX + 2, :].rearrange("p s d -> p d s"), AX.X,
                                 ALU.add).then_inc(s_done, 1)

            def window(v, prev, nxt, nxt2):
                w, q = v.w, v.q
                S, T = MAIN_S, MAIN_T
                exponents(T, w, S)
                rescale(w, w, True, S)
                if prev:
                    route_logits(w - 1)
                messages(G[:, q, :, :], w, S)
                if prev:
                    route_best(w - 1)
                if nxt:
                    n = Win(w + 1, 1 - q, v.half + q)
                    dve.wait_ge(s_load[n.q], 16 * (n.half + 1))
                    edges_of(T, EI[:, n.q, :, :], O[:, n.q, :, :], n.w, n.w, S)
                if prev:
                    route_weights(w - 1)
                if nxt:
                    dve.wait_ge(s_gath[n.q], 16 * NT * (n.half + 1))
                    candidates(T, G[:, n.q, :, :], n.w, S)
                merge(w, w, True, S)

                def extra(n, c):
                    S, T = EXTRA_S, EXTRA_T
                    dve.wait_ge(s_xload, (n + 1) * 16)
                    edges_of(T, XEI, O[:, q, :, :], w, n, S)
                    dve.wait_ge(s_xgath, (n + 1) * (16 * NT))
                    candidates(T, G[:, q, :, :], n, S)
                    across(n, S)
                    runs(T, n, S)
                    maxima(w, n, False, S)
                    exponents(T, n, S)
                    rescale(w, n, False, S)
                    messages(G[:, q, :, :], n, S)
                    merge(w, n, False, S)

                extras(dve, most, x_no, w, extra)
                if nxt:
                    across(w + 1, S)
                finish(w, q, v.half)
                dve.wait_ge(s_x1, w + 1)
                if nxt:
                    runs(T, w + 1, S)
                if nxt:
                    maxima(w + 1, w + 1, True, S)
                if prev:
                    first_use = isinstance(v.half, int) and (w - 1) < 2
                    combine(w - 1, 1 - q, None if first_use else prev_half(v))

            def prev_half(v):
                return v.half if v.q else v.half - 1

            dve.wait_ge(s_wb, 16 * 7)
            dve.wait_ge(s_load[0], 16)
            edges_of(MAIN_T, EI[:, 0, :, :], O[:, 0, :, :], 0, 0, MAIN_S)
            dve.wait_ge(s_gath[0], 16 * NT)
            candidates(MAIN_T, G[:, 0, :, :], 0, MAIN_S)
            across(0, MAIN_S)
            runs(MAIN_T, 0, MAIN_S)
            maxima(0, 0, True, MAIN_S)
            body = window
            body(Win(0, 0, 0), False, True, True)
            body(Win(1, 1, 0), True, True, True)
            body(Win(2, 0, 1), True, True, True)
            with dve.Fori(1, (NW - 3) // 2) as i:
                body(Win(i * 2 + 1, 1, i), True, True, True)
                body(Win(i * 2 + 2, 0, i + 1), True, True, True)
            body(Win(NW - 2, 1, (NW - 2) // 2), True, True, False)
            body(Win(NW - 1, 0, (NW - 1) // 2), True, False, False)
            route_logits(NW - 1)
            route_best(NW - 1)
            route_weights(NW - 1)
            combine(NW - 1, (NW - 1) % 2, (NW - 1) // 2)

        @block.scalar
        def _(act):
            def copy(o, i):
                return nc.scalar.activation(o, i, ACT.Copy)

            for k in range(K2):
                act.dma_start(wx[:, k, 0:ROW].rearrange("p (h c) -> p h c", c=HC)[:, :, 0:C],
                              w_gnn[128 * k:128 * k + 128, :].rearrange("p (h c) -> p h c", c=C))\
                    .then_inc(s_wg, 16)
            for a, v in enumerate((att_src, att_dst)):
                act.dma_start(att[:, a, :, :].rearrange("p h c -> p (h c)"),
                              v.rearrange("h c -> (h c)").partition_broadcast(128)).then_inc(s_wg, 16)
            act.dma_start(brows[0:2 * EX, :], eb1.rearrange("e (k p) -> (e k) p", p=128)).then_inc(s_wb, 16)
            act.dma_start(brows[2 * EX:4 * EX, :], eb2.rearrange("e (k p) -> (e k) p", p=128))\
                .then_inc(s_wb, 16)
            act.dma_start(brows[4 * EX:4 * EX + 1, :], rb1.unsqueeze(0)).then_inc(s_wb, 16)
            act.dma_start(gbias[:, :], gnn_bias.partition_broadcast(NP)).then_inc(s_wb, 16)
            act.dma_start(rb2_b[:, :], rb2.partition_broadcast(NP)).then_inc(s_wb, 16)
            act.dma_start(b3[:, :], eb3).then_inc(s_wb, 16)
            act.dma_start(r1[:, :, :], rw1.rearrange("(k p) f -> p k f", p=128)).then_inc(s_wb, 16)
            act.dma_start(r2[:, :], rw2).then_inc(s_we, 16)
            for s in s_x:
                act.wait_ge(s, 32)
            for t, v in ((w1, ew1), (w2, ew2), (w3, ew3)):
                act.dma_start(t[:, :, :, :].rearrange("p e k f -> p (e k) f"),
                              v.rearrange("e (k p) f -> p (e k) f", p=128)).then_inc(s_we, 16)

            act.wait_ge(s_bct, 1)
            copy(bcols[:, :], bank(0)[:, 0:4 * EX + 1]).then_inc(s_bc, 1)

            def evacuate(t, q):
                act.wait_ge(s_xt0, t + 1)
                copy(xT[:, q, :, :].rearrange("p k n -> p (k n)"), PS[:, q, 0:K2 * NP]).then_inc(s_xe0, 1)

            evacuate(0, 0)
            with act.Fori(0, (NW - 1) // 2) as i:
                evacuate(i * 2 + 1, 1)
                evacuate(i * 2 + 2, 0)
            most = most_passes(act)
            x_no = counter(act, "x_act")
            act.wait_ge(s_bc, 1)

            def narrow(q, n, S):
                act.wait_ge(S.onehot, n + 1)
                copy(OB[:, :, :], O[:, q, :, :]).then_inc(S.ob, 1)

            def transposed(n, S):
                for g, cols in enumerate(T_GROUPS):
                    act.wait_ge(S.turned, n * NG + g + 1)
                    copy(OT[:, cols[0]:cols[-1] + 1, :].rearrange("p j e -> p (j e)"),
                         p_turned[g % 2][:, 0:128 * len(cols)]).then_inc(S.ot, 1)

            def factor(n, S):
                act.wait_ge(S.old, n + 1)
                nc.scalar.activation(fac[:, :], lold[:, :], ACT.Exp).then_inc(S.fac, 1)

            def exponentials(n, S):
                act.wait_ge(S.zed, n + 1)
                nc.scalar.activation(ev[:, :, :], lr[:, :, :], ACT.Exp).then_inc(S.ev, 1)
                act.wait_ge(S.ev, n + 1)
                copy(MSG[:, :, :].rearrange("p j (h c) -> p j h c", c=HC)[:, :, :, C],
                     ev[:, :, :]).then_inc(S.den, 1)

            def take(u, m):
                kind, e = FFN[m]
                act.wait_ge(s_piece, u * NF + m + 1)
                if kind == "turn":
                    ins = copy(xT[:, 0, :, :].rearrange("p k n -> p (k n)"), bank(m)[:, 0:K2 * NP])
                elif kind == "hidden":
                    ins = nc.scalar.activation(rhid[:, :], bank(m)[:, 0:NP], ACT.Relu,
                                               bias=bcols[:, 4 * EX:4 * EX + 1])
                elif kind == "turn_w":
                    ins = copy(wT[:, :], bank(m)[0:8, 0:NP])
                elif kind == "bias3":
                    ins = copy(terms[:, 1, :], bank(m)[0:NP, 0:D])
                elif kind == "l3":
                    ins = nc.scalar.activation(terms[:, 2 + e, :], bank(m)[0:NP, 0:D], ACT.Copy,
                                               scale=wa[:, e:e + 1])
                else:
                    for f in range(K2):
                        to = h1[:, e % 2, f, :] if kind == "l1" else h2[:, e, f, :]
                        col = (2 * EX if kind == "l2" else 0) + 2 * e + f
                        ins = nc.scalar.activation(to, bank(m)[:, f * NP:(f + 1) * NP], ACT.Relu,
                                                   bias=bcols[:, col:col + 1])
                ins.then_inc(s_fa, 1)

            def takes(u, a, b):
                for m in range(a, b):
                    if FFN[m][0] != "logits":
                        take(u, m)
                    if FFN[m] == PEX_AFTER:
                        act.wait_ge(s_lgm, u + 1)
                        nc.scalar.activation(pex[:, :], lg[:, :], ACT.Exp).then_inc(s_pex, 1)
                    if FFN[m] == E2_AFTER:
                        act.wait_ge(s_gap, u + 1)
                        nc.scalar.activation(e2[:, :], gap[:, :], ACT.Exp).then_inc(s_e2, 1)

            def window(v, prev, nxt, nxt2):
                w = v.w
                if prev:
                    takes(w - 1, 0, BEFORE_SPREAD)
                exponentials(w, MAIN_S)
                factor(w, MAIN_S)
                if prev:
                    takes(w - 1, BEFORE_SPREAD, BEFORE_SUM)

                def extra(n, c):
                    narrow(v.q, n, EXTRA_S)
                    transposed(n, EXTRA_S)
                    exponentials(n, EXTRA_S)
                    factor(n, EXTRA_S)

                extras(act, most, x_no, w, extra)
                if nxt:
                    narrow(1 - v.q, w + 1, MAIN_S)
                    transposed(w + 1, MAIN_S)
                if prev:
                    takes(w - 1, BEFORE_SUM, NF)

            narrow(0, 0, MAIN_S)
            transposed(0, MAIN_S)
            windows(window)(act)
            takes(NW - 1, 0, NF)

        @block.tensor
        def _(pe):
            mm = nc.tensor.matmul
            pe.wait_ge(s_const, 11)
            pe.wait_ge(s_descents, 1)
            mm(bank(2)[0:1, 0:1], descended[:, :], ones[:, 0:1], start=True, stop=True).then_inc(s_descsum, 1)
            pe.wait_ge(s_bounds, 1)
            mm(PS[0:1, 4, 0:2 * NW], ones[:, 0:1], bounds[:, :, :].rearrange("p k w -> p (k w)"), start=True,
               stop=True).then_inc(s_span, 1)
            pe.wait_ge(s_wb, 16 * 7)
            nc.tensor.transpose(bank(0)[:, 0:4 * EX + 1], brows[:, :], ident[0:4 * EX + 1, 0:4 * EX + 1])\
                .then_inc(s_bct, 1)
            pe.wait_ge(s_wx, 2 * K2)

            def turn(t, q):
                pe.wait_ge(s_xn0, t + 1)
                for k in range(K2):
                    last = nc.tensor.transpose(PS[:, q, k * NP:(k + 1) * NP], xn[:, q, 128 * k:128 * k + 128],
                                               ident[0:NP, 0:NP])
                last.then_inc(s_xt0, 1)

            def product(t, q):
                pe.wait_ge(s_xe0, t + 1)
                for k in range(K2):
                    last = mm(PS[0:NP, 2 + q, 0:ROW + H], xT[:, q, k, :], wx[:, k, :], start=(k == 0),
                              stop=(k == K2 - 1))
                last.then_inc(s_h0, 1)

            turn(0, 0)
            turn(1, 1)
            product(0, 0)
            pe.wait_ge(s_xe0, 1)
            turn(2, 0)
            product(1, 1)
            with pe.Fori(1, (NW - 1) // 2) as i:
                pe.wait_ge(s_xe0, i * 2)
                turn(i * 2 + 1, 1)
                pe.wait_ge(s_hs, i * 2 - 1)
                product(i * 2, 0)
                pe.wait_ge(s_xe0, i * 2 + 1)
                turn(i * 2 + 2, 0)
                pe.wait_ge(s_hs, i * 2)
                product(i * 2 + 1, 1)
            pe.wait_ge(s_hs, NW - 2)
            product(NW - 1, 0)

            most = most_passes(pe)
            x_no = counter(pe, "x_pe")
            pe.wait_ge(s_hs, NW)
            pe.wait_ge(s_bc, 1)
            pe.wait_ge(s_xe0, NW)

            def transposed(n, S):
                pe.wait_ge(S.ob, n + 1)
                for g, cols in enumerate(T_GROUPS):
                    if g >= 2:
                        pe.wait_ge(S.ot, n * NG + (g - 1))
                    for k, j in enumerate(cols):
                        last = nc.tensor.transpose(p_turned[g % 2][:, 128 * k:128 * k + 128], OB[:, j, :],
                                                   ident_b[:, :])
                    last.then_inc(S.turned, 1)

            def to_row(t, n, S):
                pe.wait_ge(S.cand, n + 1)
                for k in range(2):
                    for v in range(2):
                        last = nc.tensor.transpose(p_row[:, v, k:256:2], t["cand"][:, k, v, :], ident[:, :])
                last.then_inc(S.row, 1)

            def from_row(n, S):
                pe.wait_ge(S.ends, n + 1)
                for k in range(2):
                    mm(p_back[:, k, 0:H], row_run[:, k:256:2], ident[0:H, 0:H], start=True, stop=True)
                    last = mm(p_back[:, k, H:H + 1], row_end[0:1, k:256:2], ident[0:1, 0:1], start=True, stop=True)
                last.then_inc(S.back, 1)

            def maxima(t, n, S):
                pe.wait_ge(S.mid, n + 1)
                cols = list(range(NT)) + [0, NT - 1]
                for i, j in enumerate(cols):
                    last = mm(p_mid, OB[:, j, :], t["mid_b"][:, i, :, :].rearrange("p s c -> p (s c)"),
                              start=(i == 0), stop=(i == len(cols) - 1))
                last.then_inc(S.mids, 1)

            def spread(n, S):
                pe.wait_ge(S.nval, n + 1)
                pe.wait_ge(S.ot, (n + 1) * NG)
                for j in range(NT):
                    last = mm(p_spread[:, j, :, :].rearrange("p s c -> p (s c)"), OT[:, j, :],
                              nval_b[:, :, :, :].rearrange("p s k h -> p (s k h)"), start=True, stop=True)
                last.then_inc(S.spread, 1)

            def aggregate(q, n, S):
                pe.wait_ge(S.msg, n + 1)
                pe.wait_ge(S.den, n + 1)
                for j in range(NT):
                    last = mm(p_sum, O[:, q, j, :], MSG[:, j, :], start=(j == 0), stop=(j == NT - 1))
                last.then_inc(S.agg, 1)

            def pieces(u, a, b, first=False):
                for m in range(a, b):
                    kind, e = FFN[m]
                    if m == piece("logits") + 3:
                        pe.wait_ge(s_fd, u + 1)
                    elif m >= 3:
                        pe.wait_ge(s_fa, u * N_FA + taken(m - 3))
                    elif m == 0 and not first:
                        pe.wait_ge(s_fa, u * N_FA)
                    ps = bank(m)

                    def ready(kind2, e2=0):
                        pe.wait_ge(s_fa, u * N_FA + taken(piece(kind2, e2)))

                    if kind == "turn":
                        pe.wait_ge(s_x1, u + 1)
                        for k in range(K2):
                            last = nc.tensor.transpose(ps[:, k * NP:(k + 1) * NP],
                                                       xn[:, 0, 128 * k:128 * k + 128], ident[0:NP, 0:NP])
                    elif kind == "hidden":
                        ready("turn")
                        for k in range(K2):
                            last = mm(ps[:, 0:NP], r1[:, k, :], xT[:, 0, k, :], start=(k == 0), stop=(k == 1))
                    elif kind == "logits":
                        ready("hidden")
                        last = mm(ps[0:NP, 0:EX], rhid[:, :], r2[:, :], start=True, stop=True)
                    elif kind in ("l1", "l2"):
                        ready(*(("turn",) if kind == "l1" else ("l1", e)))
                        wt, act_in = (w1, xT[:, 0, :, :]) if kind == "l1" else (w2, h1[:, e % 2, :, :])
                        for f in range(K2):
                            for k in range(K2):
                                last = mm(ps[:, f * NP:(f + 1) * NP], wt[:, e, k, 128 * f:128 * f + 128],
                                          act_in[:, k, :], start=(k == 0), stop=(k == 1))
                    elif kind == "turn_w":
                        pe.wait_ge(s_wts, u + 1)
                        last = nc.tensor.transpose(ps[0:8, 0:NP], wa[:, :], ident[0:NP, 0:NP])
                    elif kind == "bias3":
                        ready("turn_w")
                        last = mm(ps[0:NP, 0:D], wT[0:EX, :], b3[:, :], start=True, stop=True)
                    else:
                        ready("l2", e)
                        for k in range(K2):
                            last = mm(ps[0:NP, 0:D], h2[:, e, k, :], w3[:, e, k, :], start=(k == 0),
                                      stop=(k == 1))
                    last.then_inc(s_piece, 1)

            pe.wait_ge(s_we, 64)

            def window(v, prev, nxt, nxt2):
                w, q = v.w, v.q
                first = isinstance(w, int) and w == 1
                if prev:
                    pieces(w - 1, 0, BEFORE_SPREAD, first)
                spread(w, MAIN_S)
                if prev:
                    pieces(w - 1, BEFORE_SPREAD, BEFORE_SUM)
                aggregate(q, w, MAIN_S)

                def extra(n, c):
                    to_row(EXTRA_T, n, EXTRA_S)
                    transposed(n, EXTRA_S)
                    from_row(n, EXTRA_S)
                    maxima(EXTRA_T, n, EXTRA_S)
                    spread(n, EXTRA_S)
                    aggregate(q, n, EXTRA_S)

                extras(pe, most, x_no, w, extra)
                if nxt:
                    to_row(MAIN_T, w + 1, MAIN_S)
                    transposed(w + 1, MAIN_S)
                if prev:
                    pieces(w - 1, BEFORE_SUM, BEFORE_RUNS)
                if nxt:
                    from_row(w + 1, MAIN_S)
                if prev:
                    pieces(w - 1, BEFORE_RUNS, BEFORE_MAXIMA)
                if nxt:
                    maxima(MAIN_T, w + 1, MAIN_S)
                if prev:
                    pieces(w - 1, BEFORE_MAXIMA, NF)

            to_row(MAIN_T, 0, MAIN_S)
            transposed(0, MAIN_S)
            from_row(0, MAIN_S)
            maxima(MAIN_T, 0, MAIN_S)
            window(Win(0, 0, 0), False, True, True)
            window(Win(1, 1, 0), True, True, True)
            window(Win(2, 0, 1), True, True, True)
            with pe.Fori(1, (NW - 3) // 2) as i:
                window(Win(i * 2 + 1, 1, i), True, True, True)
                window(Win(i * 2 + 2, 0, i + 1), True, True, True)
            window(Win(NW - 2, 1, (NW - 2) // 2), True, True, False)
            window(Win(NW - 1, 0, (NW - 1) // 2), True, False, False)
            pieces(NW - 1, 0, NF)


_INS = ["x", "src", "dst", "L0_gnn_W", "L0_gnn_att_src", "L0_gnn_att_dst", "L0_gnn_bias", "L0_ffn_router_w1",
        "L0_ffn_router_b1", "L0_ffn_router_w2", "L0_ffn_router_b2", "L0_ffn_expert_w1", "L0_ffn_expert_b1",
        "L0_ffn_expert_w2", "L0_ffn_expert_b2", "L0_ffn_expert_w3", "L0_ffn_expert_b3"]


def kernel(**inputs):
    import numpy as _np
    import concourse.bacc as _bacc
    from concourse import mybir as _mybir
    from concourse.bass_utils import run_bass_kernel_spmd as _run

    nc = _bacc.Bacc("TRN2", target_bir_lowering=False, num_devices=1)
    arrays, args = {}, []
    for name in _INS:
        a = _np.ascontiguousarray(inputs[name])
        arrays[f"in_{name}_dram"] = a
        args.append(nc.dram_tensor(f"in_{name}_dram", a.shape, _mybir.dt.from_np(a.dtype), kind="ExternalInput").ap())
    args.append(nc.dram_tensor("out_0_dram", (N, D), _mybir.dt.float32, kind="ExternalOutput").ap())
    gat_ffn(nc, *args)
    r = _run(nc, [arrays], core_ids=[0])
    return r.results[0]["out_0_dram"]
```

```python
import concourse.bass as bass
from concourse import mybir
from collections import namedtuple
from contextlib import ExitStack


N, D, H, C = 3125, 256, 4, 64
NW, NP = 25, 125
E_IN = 53125
NT = 18
EC = 128 * NT
BLK = 8
NCOL = 416
NB_P = NCOL // BLK
NB = 128 * NB_P
E_PAD = 128 * NCOL + EC
PAD_DST = 4095
HC = C + 1
ROW = H * HC
K2 = D // 128
EX, RH = 6, 128
BIG = 1.0e30
EPS = 1e-5
SLOPE = 0.2
PLAN_AT = 12
X_STEP = 5
STEPS = [(a, a + X_STEP) for a in range(0, NW, X_STEP)]
TABLE_STEPS = [(0, 6), (6, 12), (12, 18), (18, 23), (23, NW)]
HALVES = ((0, 112), (112, NP))
T_GROUPS = [range(g, min(g + 6, NT)) for g in range(0, NT, 6)]
PARTS = 3
NG = len(T_GROUPS)
SQ = E_IN // NP
SORT_KEYS = 3125
SORT_CHUNKS = E_IN // SORT_KEYS
KEY_STEP = 4096

FFN = [("hidden", 0), ("l1", 0), ("logits", 0), ("l1", 1), ("l2", 0), ("l1", 2), ("l2", 1),
       ("l1", 3), ("l2", 2), ("l1", 4), ("l2", 3), ("l1", 5), ("l2", 4), ("turn_w", 0), ("l2", 5),
       ("bias3", 0), ("l3", 0), ("l3", 1), ("l3", 2), ("l3", 3), ("l3", 4), ("l3", 5)]
NF = len(FFN)
FA_0 = 2
BEFORE_SPREAD, BEFORE_SUM, BEFORE_RUNS, BEFORE_MAXIMA, BEFORE_TURN = 0, 9, 14, 19, 21
BEFORE_EXP = 2
ROUTE_AFTER = ("l2", 2)

Win = namedtuple("Win", "w q half")


def piece(kind, e=0):
    return FFN.index((kind, e))


def taken(m):
    return FA_0 + m + 1


def bank_of(m):
    return 5 + (m - 1) % 3 if m else 3


def before_in_bank(m):
    return m - 3 if m > 3 else max(k for k in range(NF) if bank_of(k) == bank_of(m)) - NF


def gat_ffn(nc, x, src, dst, w_gnn, att_src, att_dst, gnn_bias, rw1, rb1, rw2, rb2,
            ew1, eb1, ew2, eb2, ew3, eb3, out):
    f32, bf16, i32, u32 = mybir.dt.float32, mybir.dt.bfloat16, mybir.dt.int32, mybir.dt.uint32
    ALU, ACT, AX = mybir.AluOpType, mybir.ActivationFunctionType, mybir.AxisListType

    ctx = ExitStack()
    with ctx:
        def sb(name, shape, dt=f32):
            return ctx.enter_context(nc.sbuf_tensor(name, shape, dt))

        def sem(name):
            return ctx.enter_context(nc.semaphore(name))

        table = nc.dram_tensor("table", (N, ROW), f32, kind="Internal").ap()
        edges = nc.dram_tensor("edges", (E_PAD, 2), i32, kind="Internal").ap()

        ident = sb("ident", [128, 128])
        ident_b = sb("ident_b", [128, 128], bf16)
        ones = sb("ones", [128, 1])
        scrap = sb("scrap", [1, 1])
        tick = sb("tick", [1, 1])
        iota_n = sb("iota_n", [128, NP])
        wbase = sb("wbase", [128, NW + 1])
        pass_step = sb("pass_step", [1, NW])
        iota_e = sb("iota_e", [NP, 8])
        wx = sb("wx", [128, K2, ROW + H])
        att = sb("att", [128, 2, H, C])
        att_tmp = sb("att_tmp", [128, H, C])
        gbias = sb("gbias", [NP, D])
        rb2_b = sb("rb2_b", [NP, EX])
        brows = sb("brows", [4 * EX + 1, 128])
        bcols = sb("bcols", [128, 4 * EX + 1])
        b3 = sb("b3", [EX, D])
        r1 = sb("r1", [128, K2, RH])
        r2 = sb("r2", [RH, EX])
        w1 = sb("w1", [128, EX, K2, D])
        w2 = sb("w2", [128, EX, K2, D])
        w3 = sb("w3", [128, EX, K2, D])
        work = sb("work", [128, max(NW * D, NT * (64 + ROW))])
        X = work[0:NP, 0:NW * D].rearrange("p (t d) -> p t d", d=D)
        xw = sb("xw", [NP, 2, D])
        HS = sb("HS", [NP, NW, ROW + H])
        EI = sb("EI", [128, 2, NT, 2], i32)
        XEI = sb("XEI", [128, NT, 2], i32)
        G = sb("G", [128, 2, NT, ROW])
        O = sb("O", [128, 2, NT, NP])
        OB = sb("OB", [128, NT, NP], bf16)
        OT = work[0:NP, 0:NT * 64].bitcast(bf16).rearrange("p (j e) -> p j e", e=128)
        MSG = work[:, NT * 64:NT * (64 + ROW)].rearrange("p (j r) -> p j r", r=ROW)

        def pass_tiles(s):
            t = {}
            for name, shape, dt in (("dstf", [128, NT], f32), ("same", [128, NT], f32), ("first", [128, NT], f32),
                                    ("inside", [128, NT], f32), ("pen", [128, H, NT], f32),
                                    ("a", [128, H, NT], f32), ("run", [128, H, NT], f32),
                                    ("fa", [128, H, NT], f32), ("cand", [128, 2, 2, H + 1], f32),
                                    ("mid", [128, NT + 2, H + 1], f32),
                                    ("mid_b", [128, NT + 2, PARTS, H + 1], bf16)):
                t[name] = sb(f"{name}_{s}", shape, dt)
            return t

        MAIN_T, EXTRA_T = pass_tiles("m"), pass_tiles("x")
        row_same = sb("row_same", [H + 1, 256])
        row_pen = sb("row_pen", [H + 1, 256])
        row_run = sb("row_run", [H + 1, 256])
        row_end = sb("row_end", [H + 1, 256])
        cmid = sb("cmid", [NP, H + 1])
        cnone = sb("cnone", [NP, 1])
        cmax = sb("cmax", [NP, H])
        nmax = sb("nmax", [NP, H])
        nval = sb("nval", [NP, 2, H])
        nv = sb("nv", [NP, 2, H])
        nval_b = sb("nval_b", [NP, PARTS, 2, H], bf16)
        spd = sb("spd", [128, NT, 2, H])
        lold = sb("lold", [NP, H])
        own = sb("own", [NP, H])
        fac = sb("fac", [NP, H])
        al = sb("al", [128, NT, H])
        lr = sb("lr", [128, NT, H])
        ev = sb("ev", [128, NT, H])
        st = sb("st", [NP, ROW])
        rden = sb("rden", [NP, H])
        gat = sb("gat", [NP, D])
        terms = sb("terms", [NP, EX + 3, D])
        xn = sb("xn", [NP, 2, D])
        stats = sb("stats", [NP, NW, 6])
        mean = sb("mean", [NP, NW])
        rs = sb("rs", [NP, NW])
        rv = sb("rv", [NP, NW])
        rt = sb("rt", [NP, NW])
        mv = sb("mv", [NP, 2])
        xT = sb("xT", [128, 2, K2, NP])
        rhid = sb("rhid", [RH, NP])
        h1 = sb("h1", [128, 2, K2, NP])
        h2 = sb("h2", [128, EX, K2, NP])
        lg = sb("lg", [NP, EX])
        lmx = sb("lmx", [NP, 1])
        pex = sb("pex", [NP, 8])
        psm = sb("psm", [NP, 1])
        top = sb("top", [NP, 8])
        topi = sb("topi", [NP, 8], u32)
        topf = sb("topf", [NP, 2])
        gap = sb("gap", [NP, 1])
        e2 = sb("e2", [NP, 1])
        pw = sb("pw", [NP, 1])
        wa = sb("wa", [NP, 8])
        wb = sb("wb", [NP, 8])
        wT = sb("wT", [8, NP])
        partial = sb("partial", [NP, 4, D])
        yo = sb("yo", [NP, 2, D])
        pairs_in = G[0:NP, 0, 0:4, :].rearrange("p a b -> p (a b)")[:, 0:2 * SQ].bitcast(i32).rearrange(
            "p (s k) -> p s k", k=2)
        src_in = G[0:NP, 1, 0:4, :].rearrange("p a b -> p (a b)")[:, 0:SQ].bitcast(i32)
        dst_in = G[0:NP, 1, 0:4, :].rearrange("p a b -> p (a b)")[:, SQ:2 * SQ].bitcast(i32)
        n_pad = E_PAD - E_IN
        pairs = G[:, 0, 4:8, :].rearrange("p a b -> p (a b)")[:, 0:2 * NCOL].bitcast(i32).rearrange(
            "p (s k) -> p s k", k=2)
        o_flat = O[:, :, :, :].rearrange("p q j n -> p (q j n)")
        below_w = o_flat[:, 0:2 * NW * NB_P].rearrange("p (k w b) -> p k w b", k=2, b=NB_P)
        pass_of = o_flat[0:1, 0:NW * NW].rearrange("p (w c) -> p w c", c=NW)
        pads = o_flat[0:3, 2 * NW * NB_P:2 * NW * NB_P + 2 * (n_pad // 3)].bitcast(i32).rearrange(
            "p (s k) -> p s k", k=2)
        next_pair = sb("next_pair", [128, 2], i32)
        descents = o_flat[:, 0:NCOL]
        descended = sb("descended", [128, 1])
        unsorted = sb("unsorted", [1, 1], i32)
        g_flat = G[0:NP, :, :, :].rearrange("p q j r -> p (q j r)")
        hs_flat = HS[:, :, :].rearrange("p w r -> p (w r)")
        keys_in = o_flat[0:NP, 0:SORT_KEYS].bitcast(i32)
        keys, key_no = hs_flat[:, 0:SORT_KEYS], hs_flat[:, SORT_KEYS:2 * SORT_KEYS]
        below = g_flat[:, NT * ROW:NT * ROW + SORT_KEYS]
        edge_no, rank, threshold, n_below, rank_i = (
            g_flat[:, 8 * ROW + i * SQ:8 * ROW + (i + 1) * SQ] for i in range(5))
        rank_i = rank_i.bitcast(i32)
        move_to = sb("move_to", [NP, 1], i32)
        move = sb("move", [NP, 2], i32)
        bounds = sb("bounds", [128, 2, NW])
        span = sb("span", [1, 2 * NW])
        n_pass = sb("n_pass", [1, NW])
        most_f = sb("most_f", [1, 1])
        plan = sb("plan", [1, 2 * NW + 1], i32)

        PS = ctx.enter_context(nc.psum_tensor("PS", [128, 8, 512], f32))
        p_turned = [PS[0:NP, b, :].bitcast(bf16) for b in (0, 1, 4)]
        p_row = PS[0:H + 1, 2, :].rearrange("p (v i) -> p v i", v=2)
        p_back = PS[:, 2, 0:2 * (H + 1)].rearrange("p (k c) -> p k c", k=2)
        p_mid = PS[0:NP, 2, 16:16 + PARTS * (H + 1)]
        p_sum = PS[0:NP, 3, 0:ROW]
        p_spread = PS[:, 4, 0:NT * PARTS * 2 * H].rearrange("p (j s c) -> p j s c", s=PARTS, c=2 * H)

        def bank(m):
            return PS[:, bank_of(m), :]

        p_input = PS[:, 3, 0:K2 * NP]
        p_first = PS[0:1, 7, 0:1]
        p_bias = PS[:, 5, 0:4 * EX + 1]

        s_const = sem("s_const")
        s_x = [sem(f"s_xin{i}") for i in range(len(STEPS))]
        s_ein = sem("s_ein")
        s_pairs = sem("s_pairs")
        s_edged = sem("s_edged")
        s_back = sem("s_back")
        s_descents = sem("s_descents")
        s_descsum = sem("s_descsum")
        s_order = sem("s_order")
        s_numbers = sem("s_numbers")
        s_keys = sem("s_keys")
        s_keys_used = sem("s_keys_used")
        s_ranks = sem("s_ranks")
        s_moved = sem("s_moved")
        s_sorted = sem("s_sorted")
        s_resorted = sem("s_resorted")
        s_wg = sem("s_wg")
        s_wb = sem("s_wb")
        s_we = sem("s_we")
        s_chain = sem("s_chain")
        s_row = sem("s_row")
        s_tick = sem("s_tick")
        s_stats = sem("s_stats")
        s_wx = sem("s_wx")
        s_bounds = sem("s_bounds")
        s_span = sem("s_span")
        s_plan = sem("s_plan")
        s_bct = sem("s_bct")
        s_xn0 = sem("s_xn0")
        s_xt0 = sem("s_xt0")
        s_xe0 = sem("s_xe0")
        s_h0 = sem("s_h0")
        s_hs = sem("s_hs")
        s_table = sem("s_table")
        s_load = [sem("s_load0"), sem("s_load1")]
        s_xw = [sem("s_xw0"), sem("s_xw1")]
        s_gath = [sem("s_gath0"), sem("s_gath1")]
        s_out = [sem("s_out0"), sem("s_out1")]
        s_x1 = sem("s_x1")
        s_input = sem("s_input")
        s_input_sb = sem("s_input_sb")
        s_piece = sem("s_piece")
        s_fa = sem("s_fa")
        s_done = sem("s_done")
        s_lgm = sem("s_lgm")
        s_pex = sem("s_pex")
        s_gap = sem("s_gap")
        s_e2 = sem("s_e2")
        s_wts = sem("s_wts")

        Sems = namedtuple("Sems", "onehot ob turned ot cand row ends back mid mids nval spread old fac zed ev den "
                                  "msg agg merged")

        def pass_sems(s):
            return Sems(*[sem(f"s_{n}_{s}") for n in Sems._fields])

        MAIN_S, EXTRA_S = pass_sems("m"), pass_sems("x")
        s_xload = sem("s_xload")
        s_xgath = sem("s_xgath")

        block = ctx.enter_context(nc.Block())

        def row(t, w):
            return t[:, bass.ds(w, 1), :].rearrange("p a d -> p (a d)")

        def most_passes(eng):
            eng.wait_ge(s_plan, 1)
            return eng.value_load(plan[0:1, 2 * NW:2 * NW + 1], min_val=1, max_val=NW)

        def is_unsorted(eng):
            eng.wait_ge(s_order, 1)
            return eng.value_load(unsorted[0:1, 0:1], min_val=0, max_val=128)

        def extras(eng, most, x, w, body):
            with eng.If(most > 1):
                n = eng.value_load(plan[0:1, bass.ds(NW + w, 1)], min_val=1, max_val=NW)
                with eng.If(n > 1):
                    with eng.Fori(1, n) as c:
                        body(eng.snap(x), c)
                        eng.reg_add(x, x, 1)

        def windows(body, peeled=0):
            def run(eng):
                body(Win(0, 0, 0), False, True, True)
                for w in range(1, 2 * peeled + 1):
                    body(Win(w, w % 2, w // 2), True, True, True)
                with eng.Fori(peeled, (NW - 3) // 2) as i:
                    body(Win(i * 2 + 1, 1, i), True, True, True)
                    body(Win(i * 2 + 2, 0, i + 1), True, True, True)
                body(Win(NW - 2, 1, (NW - 2) // 2), True, True, False)
                body(Win(NW - 1, 0, (NW - 1) // 2), True, False, False)
            return run

        def val(eng, v):
            return v if isinstance(v, int) else eng.to_reg(v)

        def counter(eng, name):
            x = eng.alloc_register(name)
            eng.reg_mov(x, 0)
            return x

        @block.sync
        def _(sp):
            sp.dma_start(src_in, src.rearrange("(p s) -> p s", p=NP)).then_inc(s_ein, 16)
            sp.dma_start(dst_in, dst.rearrange("(p s) -> p s", p=NP)).then_inc(s_ein, 16)
            xv = x.rearrange("(t p) d -> p t d", p=NP)
            def load_steps(steps):
                for c, d in steps:
                    for a, b in HALVES:
                        sp.dma_start(X[a:b, c:d, :], xv[a:b, c:d, :]).then_inc(s_x[c // X_STEP], 16)

            load_steps(STEPS[0:1])
            sp.wait_ge(s_pairs, 2)
            sp.wait_ge(s_const, 2)
            sp.dma_start(edges[0:E_IN, :].rearrange("(p s) k -> p (s k)", p=NP),
                         pairs_in.rearrange("p s k -> p (s k)")).then_inc(s_edged, 16)
            sp.dma_start(edges[E_IN:E_PAD, :].rearrange("(p s) k -> p (s k)", p=3),
                         pads[:, :, :].rearrange("p s k -> p (s k)")).then_inc(s_edged, 16)
            load_steps(STEPS[1:2])
            sp.wait_ge(s_edged, 32)
            sp.dma_start(pairs.rearrange("p s k -> p (s k)"),
                         edges[0:128 * NCOL, :].rearrange("(p s) k -> p (s k)", p=128)).then_inc(s_back, 16)
            sp.dma_start(next_pair[:, :], edges[NCOL:129 * NCOL, :].rearrange("(p s) k -> p s k", p=128)[:, 0, :])\
                .then_inc(s_back, 16)
            load_steps(STEPS[2:])
            with sp.If(is_unsorted(sp) > 0):
                with sp.Fori(0, SORT_CHUNKS) as c:
                    used, at = val(sp, c + 1), c * SORT_KEYS
                    val(sp, at * 4)
                    sp.wait_ge(s_keys_used, used)
                    sp.dma_start(keys_in, dst[bass.ds(at, SORT_KEYS)].partition_broadcast(NP)).then_inc(s_keys, 16)
                sp.wait_ge(s_sorted, 1)
                sp.dma_start(pairs.rearrange("p s k -> p (s k)"),
                             edges[0:128 * NCOL, :].rearrange("(p s) k -> p (s k)", p=128)).then_inc(s_resorted, 16)
            tv = table.rearrange("(t p) r -> p t r", p=NP)
            for c, d in TABLE_STEPS:
                sp.wait_ge(s_hs, d)
                for a, b in HALVES:
                    sp.dma_start(tv[a:b, c:d, :], HS[a:b, c:d, 0:ROW]).then_inc(s_table, 16)

            edge_list = edges.rearrange("e k -> (e k)")
            x_list, out_list = x.rearrange("n d -> (n d)"), out.rearrange("n d -> (n d)")
            most = most_passes(sp)
            x_no = counter(sp, "x_sp")

            def first_edge(w):
                return offset(sp.value_load(plan[0:1, bass.ds(w, 1)], min_val=0, max_val=2 * BLK * NB))

            def offset(v):
                val(sp, v * 4)
                return v

            def load(e0, q):
                sp.dma_start(EI[:, q, :, :].rearrange("p j k -> p (j k)"),
                             edge_list[bass.ds(e0, 2 * EC)].rearrange("(p j) -> p j", p=128))\
                    .then_inc(s_load[q], 16)

            def window(v, prev, nxt, nxt2):
                if nxt2:
                    gathered, seen = val(sp, 16 * NT * (v.half + 1)), val(sp, v.w + 1)
                    e0 = first_edge(v.w + 2)
                    sp.wait_ge(s_gath[v.q], gathered)
                    sp.wait_ge(MAIN_S.onehot, seen)
                    load(e0, v.q)

                def extra(n, c):
                    e0 = first_edge(v.w)
                    start = nc.s_assert_within(e0 + c * (2 * EC), 0, 2 * BLK * NB, skip_runtime_bounds_check_because=
                                               "a pass starts before the window's last edge")
                    start, main, before = offset(start), val(sp, v.w + 1), val(sp, n + 1)
                    sp.wait_ge(MAIN_S.merged, main)
                    sp.wait_ge(EXTRA_S.merged, before)
                    sp.dma_start(XEI[:, :, :].rearrange("p j k -> p (j k)"),
                                 edge_list[bass.ds(start, 2 * EC)].rearrange("(p j) -> p j", p=128))\
                        .then_inc(s_xload, 16)

                extras(sp, most, x_no, v.w, extra)
                if nxt:
                    if prev:
                        used = val(sp, v.w)
                    at = offset((v.w + 1) * (NP * D))
                    if prev:
                        sp.wait_ge(s_x1, used)
                    load_x(at, 1 - v.q)
                if not isinstance(v.w, int) or v.w >= 2:
                    store(v.w - 2, v.q)

            def store(w, q):
                done, at = val(sp, w + 1), offset(w * (NP * D))
                sp.wait_ge(s_done, done)
                sp.dma_start(out_list[bass.ds(at, NP * D)].rearrange("(p d) -> p d", p=NP), yo[:, q, :])\
                    .then_inc(s_out[q], 16)

            def load_x(at, q):
                sp.dma_start(xw[:, q, :], x_list[bass.ds(at, NP * D)].rearrange("(p d) -> p d", p=NP))\
                    .then_inc(s_xw[q], 16)

            load(first_edge(0), 0)
            load(first_edge(1), 1)
            load_x(0, 0)
            windows(window, 1)(sp)
            store(NW - 2, (NW - 2) % 2)
            store(NW - 1, (NW - 1) % 2)
            sp.wait_ge(s_out[0], 16 * ((NW + 1) // 2))
            sp.wait_ge(s_out[1], 16 * (NW // 2))
            sp.wait_ge(s_table, 32 * len(TABLE_STEPS))

        @block.gpsimd
        def _(pool):
            pool.memset(pads[:, :, 0:1], 0).then_inc(s_const, 1)
            pool.memset(pads[:, :, 1:2], PAD_DST).then_inc(s_const, 1)
            pool.memset(ident[:, :], 0.0).then_inc(s_const, 1)
            pool.wait_ge(s_const, 3)
            pool.affine_select(out=ident[:, :], in_=ident[:, :], compare_op=ALU.not_equal, fill=1.0, base=0,
                               pattern=[[-1, 128]], channel_multiplier=1).then_inc(s_const, 1)
            pool.wait_ge(s_const, 4)
            pool.memset(tick[:, :], 0.0).then_inc(s_const, 1)
            pool.memset(ones[:, :], 1.0).then_inc(s_const, 1)
            pool.tensor_copy(ident_b[:, :], ident[:, :]).then_inc(s_const, 1)

            def hold():
                pool.tensor_tensor(tick[:, :], tick[:, :], tick[:, :], ALU.mult).then_inc(s_tick, 1)
                pool.wait_ge(s_tick, 1)
                pool.sem_clear(s_tick)

            def count(t, step, n, base=0, mult=0):
                pool.iota(t, pattern=[[step, n]], base=base, channel_multiplier=mult,
                          allow_small_or_imprecise_dtypes=True).then_inc(s_const, 1)

            count(iota_n[:, :], 1, NP)
            count(wbase[:, :], NP, NW + 1)
            count(pass_step[:, :], EC // BLK, NW)
            count(iota_e[:, :], 1, 8)

            pool.wait_ge(s_const, 11)
            with pool.If(is_unsorted(pool) > 0):
                pool.iota(key_no, pattern=[[1, SORT_KEYS]], base=0, channel_multiplier=0,
                          allow_small_or_imprecise_dtypes=True).then_inc(s_numbers, 1)
                pool.iota(edge_no, pattern=[[1, SQ]], base=0, channel_multiplier=SQ,
                          allow_small_or_imprecise_dtypes=True).then_inc(s_numbers, 1)
                pool.wait_ge(s_ranks, 1)
                hold()
                with pool.Fori(0, SQ) as s:
                    pool.tensor_copy(move_to[:, :], rank_i[:, bass.ds(s, 1)]).then_inc(s_tick, 1)
                    pool.tensor_copy(move[:, :], pairs_in[:, bass.ds(s, 1), :].rearrange("p a k -> p (a k)"))\
                        .then_inc(s_tick, 1)
                    pool.wait_ge(s_tick, 2)
                    pool.sem_clear(s_tick)
                    pool.indirect_dma_start(edges, bass.IndirectOffsetOnAxis(ap=move_to[:, 0:1], axis=0),
                                            move[:, :], None).then_inc(s_moved, 16)
                    pool.wait_ge(s_moved, s * 16 + 16)
                    hold()
                pool.tensor_tensor(tick[:, :], tick[:, :], tick[:, :], ALU.mult).then_inc(s_sorted, 1)
            most = most_passes(pool)
            x_no = counter(pool, "x_pool")
            pool.wait_ge(s_table, 32 * len(TABLE_STEPS))

            def gather(idx, q, done):
                for j in range(NT):
                    pool.indirect_dma_start(
                        G[:, q, j, :], None, table,
                        bass.IndirectOffsetOnAxis(ap=idx[:, j, 0:1], axis=0)).then_inc(done, 16)

            def combine(u, q, half):
                terms_in = val(pool, (u + 1) * NF + FA_0)
                if not (isinstance(half, int) and half == 0):
                    kept = val(pool, half * 16)
                    pool.wait_ge(s_out[q], kept)
                    hold()
                pool.wait_ge(s_fa, terms_in)
                hold()
                four = partial[:, :, :]
                for n, (o, a, b) in enumerate((
                        (four, terms[:, q:q + 4, :], terms[:, q + 4:q + 8, :]),
                        (four[:, 0:2, :], four[:, 0:2, :], four[:, 2:4, :]))):
                    pool.tensor_tensor(o, a, b, ALU.add).then_inc(s_tick, 1)
                    pool.wait_ge(s_tick, n + 1)
                pool.sem_clear(s_tick)
                pool.tensor_tensor(yo[:, q, :], four[:, 0, :], four[:, 1, :], ALU.add).then_inc(s_done, 1)

            def window(v, prev, nxt, nxt2):
                if nxt:
                    loaded, used = val(pool, 16 * (v.half + v.q + 1)), val(pool, v.w)
                    pool.wait_ge(s_load[1 - v.q], loaded)
                    hold()
                    if prev:
                        pool.wait_ge(MAIN_S.msg, used)
                        hold()
                    gather(EI[:, 1 - v.q, :, :], 1 - v.q, s_gath[1 - v.q])

                def extra(n, c):
                    pool.wait_ge(s_xload, (n + 1) * 16)
                    hold()
                    gather(XEI, v.q, s_xgath)
                    pool.wait_ge(EXTRA_S.msg, n + 1)
                    hold()

                if not isinstance(v.w, int) or v.w >= 2:
                    combine(v.w - 2, v.q, v.half - 1)
                extras(pool, most, x_no, v.w, extra)

            pool.wait_ge(s_load[0], 16)
            gather(EI[:, 0, :, :], 0, s_gath[0])
            windows(window, 2)(pool)
            combine(NW - 2, 1, (NW - 2) // 2)

        @block.vector
        def _(dve):
            v_ = nc.vector
            links = [0]

            def link(ins):
                links[0] += 1
                ins.then_inc(s_chain, 1)
                dve.wait_ge(s_chain, links[0])

            def note(ins):
                links[0] += 1
                ins.then_inc(s_chain, 1)

            def follow():
                dve.wait_ge(s_chain, links[0])

            def tell(ins, done, n):
                ins.then_inc(done, 1)
                dve.wait_ge(done, n)

            def settle():
                link(v_.memset(scrap[:, :], 0.0))
                relink()

            def relink():
                dve.sem_clear(s_chain)
                links[0] = 0

            def rsqrt(r, var, v, t):
                link(v_.tensor_scalar(v, var, EPS, None, ALU.add))
                link(v_.tensor_scalar(r.bitcast(i32), v.bitcast(i32), -0.5, 1597463007.0, ALU.mult, ALU.add))
                link(v_.tensor_scalar(v, v, -0.5, None, ALU.mult))
                for _ in range(3):
                    link(v_.tensor_tensor(t, r, r, ALU.mult))
                    link(v_.tensor_tensor(t, t, v, ALU.mult))
                    link(v_.scalar_tensor_tensor(r, t, 1.5, r, ALU.add, ALU.mult))

            def rsqrt_column(r, var, v, t):
                link(v_.tensor_scalar(v, var, EPS, None, ALU.add))
                link(v_.tensor_scalar(r.bitcast(i32), v.bitcast(i32), -0.5, 1597463007.0, ALU.mult, ALU.add))
                link(v_.tensor_scalar(v, v, -0.5, None, ALU.mult))
                for _ in range(3):
                    link(v_.scalar_tensor_tensor(t, r, r, v, ALU.mult, ALU.mult))
                    link(v_.scalar_tensor_tensor(r, t, 1.5, r, ALU.add, ALU.mult))

            def split(parts, t, left):
                link(v_.tensor_copy(parts[0], t))
                link(v_.tensor_tensor(left, t, parts[0], ALU.subtract))
                link(v_.tensor_copy(parts[1], left))
                return lambda: v_.tensor_tensor(parts[2], left, parts[1], ALU.subtract)

            dve.wait_ge(s_ein, 32)
            tell(v_.tensor_copy(pairs_in[:, :, 0], src_in), s_pairs, 1)
            tell(v_.tensor_copy(pairs_in[:, :, 1], dst_in), s_pairs, 2)
            for t in (MAIN_T, EXTRA_T):
                link(v_.memset(t["same"][:, 0:1], 0.0))
                link(v_.memset(t["first"][:, 0:1], 1.0))
                link(v_.memset(t["cand"][:, :, 0, H:H + 1], 1.0))
                link(v_.memset(t["inside"][:, NT - 1:NT], 0.0))
            link(v_.memset(row_same[:, 0:1], 0.0))
            link(v_.memset(row_end[:, 255:256], 1.0))
            tell(v_.memset(pex[:, EX:8], -1.0), EXTRA_S.merged, 1)

            dve.wait_ge(s_wg, 64)
            for k in range(K2):
                wk = wx[:, k, 0:ROW].rearrange("p (h c) -> p h c", c=HC)
                for a in range(2):
                    link(v_.tensor_tensor(att_tmp[:, :, :], wk[:, :, 0:C], att[:, a, :, :], ALU.mult))
                    to = wk[:, :, C:HC].rearrange("p h c -> p (h c)") if a == 0 else wx[:, k, ROW:ROW + H]
                    tell(v_.tensor_reduce(to, att_tmp[:, :, :], AX.X, ALU.add), s_wx, 2 * k + a + 1)

            def statistics(steps):
                for i in steps:
                    dve.wait_ge(s_x[i], 32)
                    for t in range(*STEPS[i]):
                        v_.bn_stats(row(stats, t), row(X, t)).then_inc(s_stats, 1)

            statistics(range(0, 2))

            dve.wait_ge(s_back, 32)
            link(v_.tensor_tensor(descents[:, 1:NCOL], pairs[:, 1:NCOL, 1], pairs[:, 0:NCOL - 1, 1], ALU.is_lt))
            link(v_.tensor_tensor(descents[:, 0:1], next_pair[:, 1:2], pairs[:, NCOL - 1:NCOL, 1], ALU.is_lt))
            tell(v_.tensor_reduce(descended[:, :], descents, AX.X, ALU.max), s_descents, 1)
            dve.wait_ge(s_descsum, 1)
            tell(v_.tensor_copy(unsorted[:, :], p_first), s_order, 1)
            relink()
            with dve.If(is_unsorted(dve) > 0):
                tell(v_.memset(rank, 0.0), s_keys_used, 1)
                dve.wait_ge(s_numbers, 2)
                with dve.Fori(0, SORT_CHUNKS) as c:
                    dve.wait_ge(s_keys, c * 16 + 16)
                    tell(v_.scalar_tensor_tensor(keys, keys_in, float(KEY_STEP), key_no, ALU.mult, ALU.add),
                         s_keys_used, c + 2)
                    link(v_.tensor_scalar(threshold, edge_no, 0.0, float(KEY_STEP - 1), ALU.max, ALU.min))
                    link(v_.scalar_tensor_tensor(threshold, pairs_in[:, :, 1], float(KEY_STEP), threshold,
                                                 ALU.mult, ALU.add))
                    link(v_.tensor_scalar(edge_no, edge_no, float(SORT_KEYS), None, ALU.subtract))
                    relink()
                    with dve.Fori(0, SQ) as s:
                        link(v_.tensor_scalar(below, keys, threshold[:, bass.ds(s, 1)], None, ALU.is_lt))
                        link(v_.tensor_reduce(n_below[:, bass.ds(s, 1)], below, AX.X, ALU.add))
                        relink()
                    link(v_.tensor_tensor(rank, rank, n_below, ALU.add))
                    relink()
                tell(v_.tensor_copy(rank_i, rank), s_ranks, 1)
                dve.wait_ge(s_resorted, 16)
                settle()

            statistics(range(2, len(STEPS)))
            dve.wait_ge(s_stats, NW)
            dve.wait_ge(s_const, 11)
            link(v_.tensor_tensor(mean[:, :], stats[:, :, 1], stats[:, :, 4], ALU.add))
            link(v_.tensor_tensor(rt[:, :], stats[:, :, 1], stats[:, :, 4], ALU.subtract))
            link(v_.tensor_tensor(rt[:, :], rt[:, :], rt[:, :], ALU.mult))
            link(v_.tensor_tensor(rv[:, :], stats[:, :, 2], stats[:, :, 5], ALU.add))
            link(v_.scalar_tensor_tensor(rv[:, :], rt[:, :], float(D // 4), rv[:, :], ALU.mult, ALU.add))
            link(v_.tensor_scalar(rv[:, :], rv[:, :], 1.0 / D, None, ALU.mult))
            link(v_.tensor_scalar(mean[:, :], mean[:, :], 0.5, None, ALU.mult))
            rsqrt(rs[:, :], rv[:, :], rv[:, :], rt[:, :])
            relink()

            def normalise(t, q):
                tell(v_.tensor_scalar(xn[:, q, :], row(X, t), mean[:, bass.ds(t, 1)], rs[:, bass.ds(t, 1)],
                                 ALU.subtract, ALU.mult), s_xn0, t + 1)

            normalise(0, 0)
            normalise(1, 1)
            with dve.Fori(0, PLAN_AT // 4) as i:
                for k in range(4):
                    dve.wait_ge(s_xt0, i * 4 + k + 1)
                    normalise(i * 4 + k + 2, k % 2)
                settle()

            def compare(k):
                blocks = pairs[:, (BLK - 1, 0)[k]:NCOL:BLK, 1].unsqueeze(1).broadcast_to([128, NW, NB_P])
                limits = wbase[:, k:k + NW].unsqueeze(2).broadcast_to([128, NW, NB_P])
                link(v_.tensor_tensor(below_w[:, k, :, :], blocks, limits, ALU.is_lt))

            def count_blocks(k):
                ins = v_.tensor_reduce(bounds[:, k, :], below_w[:, k, :, :], AX.X, ALU.add)
                link(ins) if k == 0 else tell(ins, s_bounds, 1)

            def tile(t):
                dve.wait_ge(s_xt0, t - 1)
                normalise(t, t % 2)

            t0 = PLAN_AT + 2
            tile(t0)
            compare(0)
            tile(t0 + 1)
            compare(1)
            tile(t0 + 2)
            count_blocks(0)
            tile(t0 + 3)
            count_blocks(1)
            tile(t0 + 4)
            tile(t0 + 5)
            dve.wait_ge(s_span, 1)
            link(v_.tensor_copy(span[:, :], PS[0:1, 4, 0:2 * NW]))
            link(v_.tensor_tensor(n_pass[:, :], span[:, NW:2 * NW], span[:, 0:NW], ALU.subtract))
            link(v_.tensor_tensor(pass_of, pass_step[:, :].unsqueeze(1).broadcast_to([1, NW, NW]),
                                  n_pass[:, :].unsqueeze(2).broadcast_to([1, NW, NW]), ALU.is_lt))
            tile(t0 + 6)
            note(v_.tensor_scalar(plan[0:1, 0:NW], span[:, 0:NW], float(2 * BLK), None, ALU.mult))
            link(v_.tensor_reduce(n_pass[:, :], pass_of, AX.X, ALU.add))
            link(v_.tensor_scalar(n_pass[:, :], n_pass[:, :], 1.0, None, ALU.max))
            tile(t0 + 7)
            note(v_.tensor_copy(plan[0:1, NW:2 * NW], n_pass[:, :]))
            link(v_.tensor_reduce(most_f[:, :], n_pass[:, :], AX.X, ALU.max))
            relink()
            tell(v_.tensor_copy(plan[0:1, 2 * NW:2 * NW + 1], most_f[:, :]), s_plan, 1)
            for t in range(t0 + 8, NW):
                tile(t)
            dve.wait_ge(s_hs, NW)

            most = most_passes(dve)
            x_no = counter(dve, "x_dve")

            def edges_of(t, ei, o, w, n, S):
                link(v_.tensor_scalar(t["dstf"][:, :], ei[:, :, 1], wbase[:, bass.ds(w, 1)], None, ALU.subtract))
                v_.tensor_tensor(o, iota_n[:, :].unsqueeze(1).broadcast_to([128, NT, NP]),
                                 t["dstf"][:, :].unsqueeze(2).broadcast_to([128, NT, NP]),
                                 ALU.is_equal).then_inc(S.onehot, 1)
                note(v_.tensor_copy(t["cand"][:, :, 1, :],
                                    t["dstf"][:, 0:NT:NT - 1].unsqueeze(2).broadcast_to([128, 2, H + 1])))
                link(v_.tensor_tensor(t["same"][:, 1:NT], t["dstf"][:, 1:NT], t["dstf"][:, 0:NT - 1],
                                      ALU.is_equal))
                note(v_.tensor_scalar(t["pen"][:, :, :], t["same"][:, :].unsqueeze(1).broadcast_to([128, H, NT]),
                                 -1.0, BIG, ALU.add, ALU.mult))
                link(v_.tensor_tensor_scan(t["first"][:, 1:NT], t["same"][:, 1:NT], t["same"][:, 1:NT], 1.0,
                                           ALU.mult, ALU.mult))
                note(v_.tensor_scalar(t["fa"][:, :, :],
                                      t["first"][:, :].unsqueeze(1).broadcast_to([128, H, NT]),
                                      -1.0, BIG, ALU.add, ALU.mult))
                link(v_.tensor_scalar(t["inside"][:, 0:NT - 1], t["first"][:, 0:NT - 1], -1.0, None, ALU.add))
                link(v_.scalar_tensor_tensor(t["inside"][:, 0:NT - 1], t["same"][:, 1:NT], -1.0,
                                             t["inside"][:, 0:NT - 1], ALU.add, ALU.mult))

            def candidates(t, g, n, S):
                gv = g.rearrange("p j (h c) -> p h j c", c=HC)[:, :, :, C]
                note(v_.tensor_copy(t["mid"][:, 0:NT, H], t["inside"][:, :]))
                link(v_.tensor_copy(t["a"][:, :, :], gv))
                flat = "p h j -> p (h j)"
                note(v_.tensor_tensor(t["fa"][:, :, :], t["fa"][:, :, :], t["a"][:, :, :], ALU.add))
                link(v_.tensor_tensor_scan(t["run"][:, :, :].rearrange(flat), t["pen"][:, :, :].rearrange(flat),
                                           t["a"][:, :, :].rearrange(flat), -BIG, ALU.add, ALU.max))
                link(v_.tensor_copy(t["cand"][:, 1, 0, 0:H], t["run"][:, :, NT - 1]))
                v_.tensor_reduce(t["cand"][:, 0, 0, 0:H], t["fa"][:, :, :], AX.X, ALU.max).then_inc(S.cand, 1)
                link(v_.tensor_tensor(t["mid"][:, 0:NT, 0:H], t["run"][:, :, :].rearrange("p h j -> p j h"),
                                 t["inside"][:, :].unsqueeze(2).broadcast_to([128, NT, H]), ALU.mult))

            def across(n, S, k):
                values, nodes = p_row[:, 0, :], p_row[:, 1, :]
                if k == 0:
                    dve.wait_ge(S.row, n + 1)
                    ins = v_.tensor_copy(row_run[:, :], nodes)
                elif k == 1:
                    dve.wait_ge(s_row, 1)
                    ins = v_.tensor_tensor(row_same[:, 1:256], row_run[:, 1:256], row_run[:, 0:255], ALU.is_equal)
                elif k == 2:
                    dve.wait_ge(s_row, 2)
                    ins = v_.tensor_scalar(row_pen[:, :], row_same[:, :], -1.0, BIG, ALU.add, ALU.mult)
                elif k == 3:
                    ins = v_.tensor_scalar(row_end[:, 0:255], row_same[:, 1:256], -1.0, 1.0, ALU.mult, ALU.add)
                elif k == 4:
                    dve.wait_ge(s_row, 4)
                    ins = v_.tensor_tensor_scan(row_run[:, :], row_pen[:, :], values, -BIG, ALU.add, ALU.max)
                elif k == 5:
                    dve.wait_ge(s_row, 5)
                    dve.sem_clear(s_row)
                    v_.tensor_tensor(row_run[:, :], row_run[:, :], row_end[:, :], ALU.mult).then_inc(S.ends, 1)
                    return
                ins.then_inc(s_row, 1)

            def runs(t, n, S):
                dve.wait_ge(S.back, n + 1)
                link(v_.tensor_copy(t["mid"][:, NT:NT + 2, :], p_back))
                parts = [t["mid_b"][:, :, s, :] for s in range(PARTS)]
                tell(split(parts, t["mid"][:, :, :], t["mid"][:, :, :])(), S.mid, n + 1)

            def maxima(w, n, first, S):
                hs = row(HS, w)
                a_dst = hs[:, ROW:ROW + H]
                old = hs[:, 0:ROW].rearrange("p (h c) -> p h c", c=HC)[:, :, C] if first else nmax[:, :]
                if not first:
                    link(v_.tensor_copy(lold[:, :], nval[:, 1, :]))
                note(v_.tensor_copy(nval[:, 0, :], a_dst))
                dve.wait_ge(S.mids, n + 1)
                link(v_.tensor_reduce(cmid[:, :], p_mid.rearrange("p (s c) -> p c s", s=PARTS), AX.X, ALU.add))
                link(v_.tensor_scalar(cnone[:, :], cmid[:, H:H + 1], -1.0, BIG, ALU.add, ALU.mult))
                link(v_.scalar_tensor_tensor(nmax[:, :], cmid[:, 0:H], cnone[:, :], old, ALU.add, ALU.max))
                link(v_.tensor_tensor(cmax[:, :], nmax[:, :], a_dst, ALU.add))
                link(v_.scalar_tensor_tensor(nval[:, 1, :], cmax[:, :], SLOPE, cmax[:, :], ALU.mult, ALU.max))
                lo = split([nval_b[:, s, :, :] for s in range(PARTS)], nval[:, :, :], nv[:, :, :])
                relink()
                lo().then_inc(S.nval, 1)

            def exponents(t, w, n, first, S):
                hs = row(HS, w)
                a_src = hs[:, 0:ROW].rearrange("p (h c) -> p h c", c=HC)[:, :, C]
                if first:
                    link(v_.tensor_tensor(own[:, :], a_src, hs[:, ROW:ROW + H], ALU.add))
                    note(v_.scalar_tensor_tensor(lold[:, :], own[:, :], SLOPE, own[:, :], ALU.mult, ALU.max))
                dve.wait_ge(S.spread, n + 1)
                link(v_.tensor_reduce(spd[:, :, :, :].rearrange("p j k h -> p j (k h)"),
                                      p_spread.rearrange("p j s c -> p j c s"), AX.X, ALU.add))
                v_.tensor_tensor(lold[:, :], lold[:, :], nval[:, 1, :], ALU.subtract).then_inc(S.old, 1)
                link(v_.tensor_tensor(al[:, :, :], t["a"][:, :, :].rearrange("p h j -> p j h"),
                                      spd[:, :, 0, :], ALU.add))
                link(v_.scalar_tensor_tensor(lr[:, :, :], al[:, :, :], SLOPE, al[:, :, :], ALU.mult, ALU.max))
                link(v_.tensor_tensor(lr[:, :, :], lr[:, :, :], spd[:, :, 1, :], ALU.subtract))
                v_.tensor_scalar(lr[:, :, :], lr[:, :, :], 0.0, None, ALU.min).then_inc(S.zed, 1)

            def messages(g, n, S):
                dve.wait_ge(S.ev, n + 1)
                v_.tensor_tensor(MSG[:, :, :].rearrange("p j (h c) -> p (j h) c", c=HC)[:, :, 0:C],
                                 g.rearrange("p j (h c) -> p (j h) c", c=HC)[:, :, 0:C],
                                 ev[:, :, :].rearrange("p j h -> p (j h)").unsqueeze(2)
                                 .broadcast_to([128, NT * H, C]), ALU.mult).then_inc(S.msg, 1)

            def merge(w, n, first, S):
                dve.wait_ge(S.fac, n + 1)
                s3 = st[:, :].rearrange("p (h c) -> p h c", c=HC)
                old = row(HS, w)[:, 0:ROW].rearrange("p (h c) -> p h c", c=HC) if first else s3
                n_c = C if first else HC
                if first:
                    note(v_.tensor_copy(s3[:, :, C], fac[:, :]))
                link(v_.tensor_tensor(s3[:, :, 0:n_c], old[:, :, 0:n_c],
                                      fac[:, :].unsqueeze(2).broadcast_to([NP, H, n_c]), ALU.mult))
                relink()
                dve.wait_ge(S.agg, n + 1)
                v_.tensor_tensor(st[:, :], st[:, :], p_sum, ALU.add).then_inc(S.merged, 1)
                if not first:
                    dve.wait_ge(S.merged, n + 2)
                    settle()

            def finish(w, q, half, nxt):
                def step(ins, k=None):
                    note(ins)
                    if k is not None and nxt:
                        across(w + 1, MAIN_S, k)
                    follow()

                dve.wait_ge(MAIN_S.merged, w + 1)
                s3 = st[:, :].rearrange("p (h c) -> p h c", c=HC)
                step(v_.tensor_scalar(rden[:, :], s3[:, :, C], 1e-16, None, ALU.add), 0)
                step(v_.reciprocal(rden[:, :], rden[:, :]), 1)
                step(v_.tensor_tensor(gat[:, :].rearrange("p (h c) -> p h c", c=C), s3[:, :, 0:C],
                                      rden[:, :].unsqueeze(2).broadcast_to([NP, H, C]), ALU.mult), 2)
                step(v_.tensor_tensor(gat[:, :], gat[:, :], gbias[:, :], ALU.add), 3)
                dve.wait_ge(s_xw[q], 16 * (half + 1))
                x1 = terms[:, q * (EX + 2), :]
                if not (isinstance(w, int) and w < 2):
                    dve.wait_ge(s_done, w - 1)
                step(v_.scalar_tensor_tensor(x1, gat[:, :], 0.0, xw[:, q, :], ALU.max, ALU.add), 4)
                step(v_.bn_stats(stats[:, 0, :], x1), 5)
                step(v_.bn_aggr(mv[:, :], stats[:, 0, :]))
                rsqrt_column(rs[:, 0:1], mv[:, 1:2], rv[:, 0:1], rt[:, 0:1])
                relink()
                v_.tensor_scalar(xn[:, 0, :], x1, mv[:, 0:1], rs[:, 0:1],
                                 ALU.subtract, ALU.mult).then_inc(s_x1, 1)

            def route_logits(u):
                dve.wait_ge(s_fa, u * NF + taken(piece("logits")))
                link(v_.tensor_tensor(lg[:, :], lg[:, :], rb2_b[:, :], ALU.add))
                link(v_.tensor_reduce(lmx[:, :], lg[:, :], AX.X, ALU.max))
                tell(v_.tensor_scalar(lg[:, :], lg[:, :], lmx[:, :], None, ALU.subtract), s_lgm, u + 1)

            def route_best(u):
                dve.wait_ge(s_pex, u + 1)
                note(v_.tensor_reduce(psm[:, :], pex[:, 0:EX], AX.X, ALU.add))
                link(v_.max(top[:, :], pex[:, :]))
                note(v_.reciprocal(psm[:, :], psm[:, :]))
                note(v_.max_index(topi[:, :], top[:, :], pex[:, :]))
                link(v_.tensor_tensor(gap[:, :], top[:, 1:2], top[:, 0:1], ALU.subtract))
                v_.tensor_tensor(gap[:, :], gap[:, :], psm[:, :], ALU.mult).then_inc(s_gap, 1)
                link(v_.tensor_copy(topf[:, :], topi[:, 0:2]))

            def route_weights(u):
                link(v_.tensor_scalar(wb[:, :], iota_e[:, :], topf[:, 0:1], None, ALU.is_equal))
                dve.wait_ge(s_e2, u + 1)
                note(v_.tensor_scalar(pw[:, :], e2[:, :], 1.0, None, ALU.add))
                link(v_.tensor_scalar(wa[:, :], iota_e[:, :], topf[:, 1:2], e2[:, :], ALU.is_equal, ALU.mult))
                note(v_.reciprocal(pw[:, :], pw[:, :]))
                link(v_.tensor_tensor(wa[:, :], wa[:, :], wb[:, :], ALU.add))
                tell(v_.tensor_scalar(wa[:, :], wa[:, :], pw[:, :], None, ALU.mult), s_wts, u + 1)

            def combine_last():
                u, q = NW - 1, (NW - 1) % 2
                dve.wait_ge(s_fa, NW * NF + FA_0)
                dve.wait_ge(s_done, NW - 1)
                dve.wait_ge(s_out[q], 16 * (u // 2))
                v_.tensor_reduce(yo[:, q, :], terms[:, q:q + EX + 2, :].rearrange("p s d -> p d s"), AX.X,
                                 ALU.add).then_inc(s_done, 1)

            def window(v, prev, nxt, nxt2):
                w, q = v.w, v.q
                S, T = MAIN_S, MAIN_T
                exponents(T, w, w, True, S)
                messages(G[:, q, :, :], w, S)
                if prev:
                    route_logits(w - 1)
                if nxt:
                    n = Win(w + 1, 1 - q, v.half + q)
                    dve.wait_ge(s_load[n.q], 16 * (n.half + 1))
                    edges_of(T, EI[:, n.q, :, :], O[:, n.q, :, :], n.w, n.w, S)
                if prev:
                    route_best(w - 1)
                if nxt:
                    dve.wait_ge(s_gath[n.q], 16 * NT * (n.half + 1))
                    candidates(T, G[:, n.q, :, :], n.w, S)
                if prev:
                    route_weights(w - 1)
                merge(w, w, True, S)

                def extra(n, c):
                    S, T = EXTRA_S, EXTRA_T
                    dve.wait_ge(s_xload, (n + 1) * 16)
                    edges_of(T, XEI, O[:, q, :, :], w, n, S)
                    dve.wait_ge(s_xgath, (n + 1) * (16 * NT))
                    candidates(T, G[:, q, :, :], n, S)
                    for k in range(6):
                        across(n, S, k)
                    dve.wait_ge(S.ends, n + 1)
                    runs(T, n, S)
                    maxima(w, n, False, S)
                    exponents(T, w, n, False, S)
                    messages(G[:, q, :, :], n, S)
                    merge(w, n, False, S)

                extras(dve, most, x_no, w, extra)
                finish(w, q, v.half, nxt)
                dve.wait_ge(s_x1, w + 1)
                if nxt:
                    runs(T, w + 1, S)
                    maxima(w + 1, w + 1, True, S)

            dve.wait_ge(s_wb, 16 * 7)
            dve.wait_ge(s_load[0], 16)
            edges_of(MAIN_T, EI[:, 0, :, :], O[:, 0, :, :], 0, 0, MAIN_S)
            dve.wait_ge(s_gath[0], 16 * NT)
            candidates(MAIN_T, G[:, 0, :, :], 0, MAIN_S)
            for k in range(6):
                across(0, MAIN_S, k)
            runs(MAIN_T, 0, MAIN_S)
            maxima(0, 0, True, MAIN_S)
            windows(window, 1)(dve)
            route_logits(NW - 1)
            route_best(NW - 1)
            route_weights(NW - 1)
            combine_last()

        @block.scalar
        def _(act):
            def copy(o, i):
                return nc.scalar.activation(o, i, ACT.Copy)

            for k in range(K2):
                act.dma_start(wx[:, k, 0:ROW].rearrange("p (h c) -> p h c", c=HC)[:, :, 0:C],
                              w_gnn[128 * k:128 * k + 128, :].rearrange("p (h c) -> p h c", c=C))\
                    .then_inc(s_wg, 16)
            for a, v in enumerate((att_src, att_dst)):
                act.dma_start(att[:, a, :, :].rearrange("p h c -> p (h c)"),
                              v.rearrange("h c -> (h c)").partition_broadcast(128)).then_inc(s_wg, 16)
            act.dma_start(brows[0:2 * EX, :], eb1.rearrange("e (k p) -> (e k) p", p=128)).then_inc(s_wb, 16)
            act.dma_start(brows[2 * EX:4 * EX, :], eb2.rearrange("e (k p) -> (e k) p", p=128))\
                .then_inc(s_wb, 16)
            act.dma_start(brows[4 * EX:4 * EX + 1, :], rb1.unsqueeze(0)).then_inc(s_wb, 16)
            act.dma_start(gbias[:, :], gnn_bias.partition_broadcast(NP)).then_inc(s_wb, 16)
            act.dma_start(rb2_b[:, :], rb2.partition_broadcast(NP)).then_inc(s_wb, 16)
            act.dma_start(b3[:, :], eb3).then_inc(s_wb, 16)
            act.dma_start(r1[:, :, :], rw1.rearrange("(k p) f -> p k f", p=128)).then_inc(s_wb, 16)
            act.dma_start(r2[:, :], rw2).then_inc(s_we, 16)
            for s in s_x:
                act.wait_ge(s, 32)
            for t, v in ((w1, ew1), (w2, ew2), (w3, ew3)):
                act.dma_start(t[:, :, :, :].rearrange("p e k f -> p (e k) f"),
                              v.rearrange("e (k p) f -> p (e k) f", p=128)).then_inc(s_we, 16)

            act.wait_ge(s_bct, 1)
            for a, b in ((0, 4 * EX), (4 * EX, 4 * EX + 1)):
                copy(bcols[:, a:b], p_bias[:, a:b]).then_inc(s_fa, 1)

            def evacuate(t, q):
                act.wait_ge(s_xt0, t + 1)
                copy(xT[:, q, :, :].rearrange("p k n -> p (k n)"), PS[:, q, 0:K2 * NP]).then_inc(s_xe0, 1)

            def keep_h(t, q):
                act.wait_ge(s_h0, t + 1)
                copy(row(HS, t), PS[0:NP, 2 + q, 0:ROW + H]).then_inc(s_hs, 1)

            evacuate(0, 0)
            with act.Fori(0, (NW - 1) // 2) as i:
                evacuate(i * 2 + 1, 1)
                keep_h(i * 2, 0)
                evacuate(i * 2 + 2, 0)
                keep_h(i * 2 + 1, 1)
            keep_h(NW - 1, 0)
            most = most_passes(act)
            x_no = counter(act, "x_act")
            act.wait_ge(s_fa, FA_0)

            def narrow(q, n, S):
                act.wait_ge(S.onehot, n + 1)
                copy(OB[:, :, :], O[:, q, :, :]).then_inc(S.ob, 1)

            def transposed(n, S):
                for g, cols in enumerate(T_GROUPS):
                    act.wait_ge(S.turned, n * NG + g + 1)
                    copy(OT[:, cols[0]:cols[-1] + 1, :].rearrange("p j e -> p (j e)"),
                         p_turned[g][:, 0:128 * len(cols)]).then_inc(S.ot, 1)

            def factor(n, S):
                act.wait_ge(S.old, n + 1)
                nc.scalar.activation(fac[:, :], lold[:, :], ACT.Exp).then_inc(S.fac, 1)

            def exponentials(n, S):
                act.wait_ge(S.zed, n + 1)
                nc.scalar.activation(ev[:, :, :], lr[:, :, :], ACT.Exp).then_inc(S.ev, 1)
                act.wait_ge(S.ev, n + 1)
                copy(MSG[:, :, :].rearrange("p j (h c) -> p j h c", c=HC)[:, :, :, C],
                     ev[:, :, :]).then_inc(S.den, 1)

            def take(u, m):
                kind, e = FFN[m]
                act.wait_ge(s_piece, u * NF + m + 1)
                if kind == "hidden":
                    ins = nc.scalar.activation(rhid[:, :], bank(m)[:, 0:NP], ACT.Relu,
                                               bias=bcols[:, 4 * EX:4 * EX + 1])
                elif kind == "logits":
                    ins = copy(lg[:, :], bank(m)[0:NP, 0:EX])
                elif kind == "turn_w":
                    ins = copy(wT[:, :], bank(m)[0:8, 0:NP])
                elif kind == "bias3":
                    if not (isinstance(u, int) and u == 0):
                        act.wait_ge(s_done, u)
                    ins = copy(terms[:, 1, :], bank(m)[0:NP, 0:D])
                elif kind == "l3":
                    ins = nc.scalar.activation(terms[:, 2 + e, :], bank(m)[0:NP, 0:D], ACT.Copy,
                                               scale=wa[:, e:e + 1])
                else:
                    for f in range(K2):
                        to = h1[:, e % 2, f, :] if kind == "l1" else h2[:, e, f, :]
                        col = (2 * EX if kind == "l2" else 0) + 2 * e + f
                        ins = nc.scalar.activation(to, bank(m)[:, f * NP:(f + 1) * NP], ACT.Relu,
                                                   bias=bcols[:, col:col + 1])
                ins.then_inc(s_fa, 1)

            def take_input(u):
                act.wait_ge(s_input, u + 1)
                copy(xT[:, 0, :, :].rearrange("p k n -> p (k n)"), p_input).then_inc(s_input_sb, 1)

            def takes(u, a, b):
                for m in range(a, b):
                    take(u, m)
                    if FFN[m] == ROUTE_AFTER:
                        act.wait_ge(s_lgm, u + 1)
                        nc.scalar.activation(pex[:, 0:EX], lg[:, :], ACT.Exp).then_inc(s_pex, 1)
                        act.wait_ge(s_gap, u + 1)
                        nc.scalar.activation(e2[:, :], gap[:, :], ACT.Exp).then_inc(s_e2, 1)

            def window(v, prev, nxt, nxt2):
                w = v.w
                if prev:
                    takes(w - 1, 0, BEFORE_EXP)
                exponentials(w, MAIN_S)
                factor(w, MAIN_S)
                if prev:
                    takes(w - 1, BEFORE_EXP, BEFORE_SUM)

                def extra(n, c):
                    narrow(v.q, n, EXTRA_S)
                    transposed(n, EXTRA_S)
                    exponentials(n, EXTRA_S)
                    factor(n, EXTRA_S)

                extras(act, most, x_no, w, extra)
                if nxt:
                    narrow(1 - v.q, w + 1, MAIN_S)
                    transposed(w + 1, MAIN_S)
                if prev:
                    takes(w - 1, BEFORE_SUM, BEFORE_TURN)
                take_input(w)
                if prev:
                    takes(w - 1, BEFORE_TURN, NF)

            narrow(0, 0, MAIN_S)
            transposed(0, MAIN_S)
            windows(window)(act)
            takes(NW - 1, 0, NF)

        @block.tensor
        def _(pe):
            mm = nc.tensor.matmul
            pe.wait_ge(s_const, 11)
            pe.wait_ge(s_descents, 1)
            mm(p_first, descended[:, :], ones[:, :], start=True, stop=True).then_inc(s_descsum, 1)
            pe.wait_ge(s_wb, 16 * 7)
            nc.tensor.transpose(p_bias, brows[:, :], ident[0:4 * EX + 1, 0:4 * EX + 1])\
                .then_inc(s_bct, 1)
            pe.wait_ge(s_wx, 2 * K2)

            def turn(t, q):
                pe.wait_ge(s_xn0, t + 1)
                for k in range(K2):
                    last = nc.tensor.transpose(PS[:, q, k * NP:(k + 1) * NP], xn[:, q, 128 * k:128 * k + 128],
                                               ident[0:NP, 0:NP])
                last.then_inc(s_xt0, 1)

            def product(t, q):
                pe.wait_ge(s_xe0, t + 1)
                for k in range(K2):
                    last = mm(PS[0:NP, 2 + q, 0:ROW + H], xT[:, q, k, :], wx[:, k, :], start=(k == 0),
                              stop=(k == K2 - 1))
                last.then_inc(s_h0, 1)

            turn(0, 0)
            turn(1, 1)
            product(0, 0)
            pe.wait_ge(s_xe0, 1)
            turn(2, 0)
            product(1, 1)
            def pairs_of_tiles(a, b):
                with pe.Fori(a, b) as i:
                    pe.wait_ge(s_xe0, i * 2)
                    turn(i * 2 + 1, 1)
                    pe.wait_ge(s_hs, i * 2 - 1)
                    product(i * 2, 0)
                    pe.wait_ge(s_xe0, i * 2 + 1)
                    turn(i * 2 + 2, 0)
                    pe.wait_ge(s_hs, i * 2)
                    product(i * 2 + 1, 1)

            pairs_of_tiles(1, PLAN_AT // 2 + 3)
            pe.wait_ge(s_bounds, 1)
            mm(PS[0:1, 4, 0:2 * NW], ones[:, :], bounds[:, :, :].rearrange("p k w -> p (k w)"), start=True,
               stop=True).then_inc(s_span, 1)
            pairs_of_tiles(PLAN_AT // 2 + 3, (NW - 1) // 2)
            pe.wait_ge(s_hs, NW - 2)
            product(NW - 1, 0)

            most = most_passes(pe)
            x_no = counter(pe, "x_pe")
            pe.wait_ge(s_hs, NW)
            pe.wait_ge(s_fa, FA_0)
            pe.wait_ge(s_xe0, NW)

            def transposed(n, S):
                pe.wait_ge(S.ob, n + 1)
                for g, cols in enumerate(T_GROUPS):
                    for k, j in enumerate(cols):
                        last = nc.tensor.transpose(p_turned[g][:, 128 * k:128 * k + 128], OB[:, j, :],
                                                   ident_b[:, :])
                    last.then_inc(S.turned, 1)

            def to_row(t, n, S):
                pe.wait_ge(S.cand, n + 1)
                for k in range(2):
                    for v in range(2):
                        last = nc.tensor.transpose(p_row[:, v, k:256:2], t["cand"][:, k, v, :], ident[:, :])
                last.then_inc(S.row, 1)

            def from_row(n, S):
                pe.wait_ge(S.ends, n + 1)
                for k in range(2):
                    last = mm(p_back[:, k, :], row_run[:, k:256:2], ident[0:H + 1, 0:H + 1], start=True, stop=True)
                last.then_inc(S.back, 1)

            def maxima(t, n, S):
                pe.wait_ge(S.mid, n + 1)
                cols = list(range(NT)) + [0, NT - 1]
                for i, j in enumerate(cols):
                    last = mm(p_mid, OB[:, j, :], t["mid_b"][:, i, :, :].rearrange("p s c -> p (s c)"),
                              start=(i == 0), stop=(i == len(cols) - 1))
                last.then_inc(S.mids, 1)

            def spread(n, S):
                pe.wait_ge(S.nval, n + 1)
                pe.wait_ge(S.ot, (n + 1) * NG)
                for j in range(NT):
                    last = mm(p_spread[:, j, :, :].rearrange("p s c -> p (s c)"), OT[:, j, :],
                              nval_b[:, :, :, :].rearrange("p s k h -> p (s k h)"), start=True, stop=True)
                last.then_inc(S.spread, 1)

            def aggregate(q, n, S):
                pe.wait_ge(S.msg, n + 1)
                pe.wait_ge(S.den, n + 1)
                for j in range(NT):
                    last = mm(p_sum, O[:, q, j, :], MSG[:, j, :], start=(j == 0), stop=(j == NT - 1))
                last.then_inc(S.agg, 1)

            def pieces(u, a, b, first=False):
                for m in range(a, b):
                    kind, e = FFN[m]
                    if m > 3 or m > 0 and not first:
                        pe.wait_ge(s_fa, u * NF + taken(before_in_bank(m)))
                    ps = bank(m)

                    def ready(kind2, e2=0):
                        pe.wait_ge(s_fa, u * NF + taken(piece(kind2, e2)))

                    if kind == "hidden":
                        pe.wait_ge(s_input_sb, u + 1)
                        for k in range(K2):
                            last = mm(ps[:, 0:NP], r1[:, k, :], xT[:, 0, k, :], start=(k == 0), stop=(k == 1))
                    elif kind == "logits":
                        ready("hidden")
                        last = mm(ps[0:NP, 0:EX], rhid[:, :], r2[:, :], start=True, stop=True)
                    elif kind in ("l1", "l2"):
                        if kind == "l2":
                            ready("l1", e)
                        wt, act_in = (w1, xT[:, 0, :, :]) if kind == "l1" else (w2, h1[:, e % 2, :, :])
                        for f in range(K2):
                            for k in range(K2):
                                last = mm(ps[:, f * NP:(f + 1) * NP], wt[:, e, k, 128 * f:128 * f + 128],
                                          act_in[:, k, :], start=(k == 0), stop=(k == 1))
                    elif kind == "turn_w":
                        pe.wait_ge(s_wts, u + 1)
                        last = nc.tensor.transpose(ps[0:8, 0:NP], wa[:, :], ident[0:NP, 0:NP])
                    elif kind == "bias3":
                        ready("turn_w")
                        last = mm(ps[0:NP, 0:D], wT[0:EX, :], b3[:, :], start=True, stop=True)
                    else:
                        ready("l2", e)
                        for k in range(K2):
                            last = mm(ps[0:NP, 0:D], h2[:, e, k, :], w3[:, e, k, :], start=(k == 0),
                                      stop=(k == 1))
                    last.then_inc(s_piece, 1)

            def turn_input(u):
                pe.wait_ge(s_x1, u + 1)
                for k in range(K2):
                    last = nc.tensor.transpose(p_input[:, k * NP:(k + 1) * NP], xn[:, 0, 128 * k:128 * k + 128],
                                               ident[0:NP, 0:NP])
                last.then_inc(s_input, 1)

            pe.wait_ge(s_we, 64)

            def window(v, prev, nxt, nxt2):
                w, q = v.w, v.q
                first = isinstance(w, int) and w == 1
                if prev:
                    pieces(w - 1, 0, BEFORE_SPREAD, first)
                spread(w, MAIN_S)
                if prev:
                    pieces(w - 1, BEFORE_SPREAD, BEFORE_SUM)
                aggregate(q, w, MAIN_S)

                def extra(n, c):
                    to_row(EXTRA_T, n, EXTRA_S)
                    transposed(n, EXTRA_S)
                    from_row(n, EXTRA_S)
                    maxima(EXTRA_T, n, EXTRA_S)
                    spread(n, EXTRA_S)
                    aggregate(q, n, EXTRA_S)

                extras(pe, most, x_no, w, extra)
                if nxt:
                    to_row(MAIN_T, w + 1, MAIN_S)
                    transposed(w + 1, MAIN_S)
                if prev:
                    pieces(w - 1, BEFORE_SUM, BEFORE_RUNS)
                if nxt:
                    from_row(w + 1, MAIN_S)
                if prev:
                    pieces(w - 1, BEFORE_RUNS, BEFORE_MAXIMA)
                if nxt:
                    maxima(MAIN_T, w + 1, MAIN_S)
                if prev:
                    pieces(w - 1, BEFORE_MAXIMA, BEFORE_TURN)
                turn_input(w)
                if prev:
                    pieces(w - 1, BEFORE_TURN, NF)

            to_row(MAIN_T, 0, MAIN_S)
            transposed(0, MAIN_S)
            from_row(0, MAIN_S)
            maxima(MAIN_T, 0, MAIN_S)
            windows(window, 1)(pe)
            pieces(NW - 1, 0, NF)


_INS = ["x", "src", "dst", "L0_gnn_W", "L0_gnn_att_src", "L0_gnn_att_dst", "L0_gnn_bias", "L0_ffn_router_w1",
        "L0_ffn_router_b1", "L0_ffn_router_w2", "L0_ffn_router_b2", "L0_ffn_expert_w1", "L0_ffn_expert_b1",
        "L0_ffn_expert_w2", "L0_ffn_expert_b2", "L0_ffn_expert_w3", "L0_ffn_expert_b3"]


def kernel(**inputs):
    import numpy as _np
    import concourse.bacc as _bacc
    from concourse import mybir as _mybir
    from concourse.bass_utils import run_bass_kernel_spmd as _run

    nc = _bacc.Bacc("TRN2", target_bir_lowering=False, num_devices=1)
    arrays, args = {}, []
    for name in _INS:
        a = _np.ascontiguousarray(inputs[name])
        arrays[f"in_{name}_dram"] = a
        args.append(nc.dram_tensor(f"in_{name}_dram", a.shape, _mybir.dt.from_np(a.dtype), kind="ExternalInput").ap())
    args.append(nc.dram_tensor("out_0_dram", (N, D), _mybir.dt.float32, kind="ExternalOutput").ap())
    gat_ffn(nc, *args)
    r = _run(nc, [arrays], core_ids=[0])
    return r.results[0]["out_0_dram"]
```
